# Optimizing a Trainium2 kernel written in Bass

```python
import numpy as np
import jax
import jax.numpy as jnp

def _softmax(x, axis=-1):
    return jax.nn.softmax(x, axis=axis)

def _gelu(x):
    return jax.nn.gelu(x, approximate=True)

def _silu(x):
    return jax.nn.silu(x)

def _sigmoid(x):
    return jax.nn.sigmoid(x)

def _layernorm(x, axis=-1, eps=1e-05):
    m = jnp.mean(x, axis=axis, keepdims=True)
    v = jnp.var(x, axis=axis, keepdims=True)
    return (x - m) / jnp.sqrt(v + eps)

def _scatter_add(tgt, idx, src, axis=0):
    return tgt.at[idx].add(src)

def _segment_sum(src, seg, n):
    return jax.ops.segment_sum(src, seg, n)
kernel_name = 'mk_macaron_d1_jaxref_r8_6e96cd'

def setup_inputs(seed: int=0):
    np.random.seed(seed)
    _w = jnp.asarray

    def _L0_attn_setup():
        import jax, jax.numpy as jnp
        import numpy as np
        B, T, D = (4, 256, 256)
        HS, NH, NG = (128, 16, 4)
        R = NH // NG
        key = jax.random.key(seed)
        ks = jax.random.split(key, 8)
        s = 0.02
        return {'x': jax.random.normal(ks[0], (B, T, D), dtype=jnp.float32), 'WQ': jax.random.normal(ks[1], (HS * NH, D), dtype=jnp.float32) * s, 'bQ': jax.random.normal(ks[2], (HS * NH,), dtype=jnp.float32) * s, 'WK': jax.random.normal(ks[3], (HS * NG, D), dtype=jnp.float32) * s, 'bK': jax.random.normal(ks[4], (HS * NG,), dtype=jnp.float32) * s, 'WV': jax.random.normal(ks[5], (HS * NG, D), dtype=jnp.float32) * s, 'bV': jax.random.normal(ks[6], (HS * NG,), dtype=jnp.float32) * s, 'proj': jax.random.normal(ks[7], (HS * NH, D), dtype=jnp.float32) * s}
    _L0_attn_in = _L0_attn_setup()

    def _L0_ffn_setup():
        import jax, jax.numpy as jnp
        import numpy as np
        TOP_K = 2

        def moe_forward(x, w_gate_router, w_gate_proj, w_up_proj, w_down_proj):
            E = w_gate_router.shape[0]
            scores = jnp.einsum('bsd,ed->bse', x, w_gate_router)
            topk_scores, topk_idx = jax.lax.top_k(scores, TOP_K)
            topk_probs = jax.nn.softmax(topk_scores, axis=-1)
            weights = jnp.sum(topk_probs[..., None] * jax.nn.one_hot(topk_idx, E, dtype=x.dtype), axis=-2)
            gate = jnp.einsum('bsd,efd->bsef', x, w_gate_proj)
            up = jnp.einsum('bsd,efd->bsef', x, w_up_proj)
            hidden = jax.nn.silu(gate) * up
            out = jnp.einsum('bsef,edf,bse->bsd', hidden, w_down_proj, weights)
            return out
        key = jax.random.key(seed)
        k1, k2, k3, k4, k5 = jax.random.split(key, 5)
        B, S, D, E, F = (2, 128, 256, 8, 96)
        scale_in = 1.0 / np.sqrt(D)
        scale_ff = 1.0 / np.sqrt(F)
        return {'x': jax.random.normal(k1, (B, S, D), dtype=jnp.float32), 'w_gate_router': jax.random.normal(k2, (E, D), dtype=jnp.float32) * scale_in, 'w_gate_proj': jax.random.normal(k3, (E, F, D), dtype=jnp.float32) * scale_in, 'w_up_proj': jax.random.normal(k4, (E, F, D), dtype=jnp.float32) * scale_in, 'w_down_proj': jax.random.normal(k5, (E, D, F), dtype=jnp.float32) * scale_ff}
    _L0_ffn_in = _L0_ffn_setup()
    _d = {'L0_attn_x': _L0_attn_in['x'], 'L0_attn_WQ': _L0_attn_in['WQ'], 'L0_attn_bQ': _L0_attn_in['bQ'], 'L0_attn_WK': _L0_attn_in['WK'], 'L0_attn_bK': _L0_attn_in['bK'], 'L0_attn_WV': _L0_attn_in['WV'], 'L0_attn_bV': _L0_attn_in['bV'], 'L0_attn_proj': _L0_attn_in['proj'], 'L0_ffn_w_gate_router': _L0_ffn_in['w_gate_router'], 'L0_ffn_w_gate_proj': _L0_ffn_in['w_gate_proj'], 'L0_ffn_w_up_proj': _L0_ffn_in['w_up_proj'], 'L0_ffn_w_down_proj': _L0_ffn_in['w_down_proj']}
    _x0 = _d['L0_attn_x']
    _d['L0_attn_x'] = jax.random.normal(jax.random.fold_in(jax.random.key(seed), 1), (4, 1024, 256), dtype=_x0.dtype)
    del _x0
    return _d

def reference(L0_attn_x, L0_attn_WQ, L0_attn_bQ, L0_attn_WK, L0_attn_bK, L0_attn_WV, L0_attn_bV, L0_attn_proj, L0_ffn_w_gate_router, L0_ffn_w_gate_proj, L0_ffn_w_up_proj, L0_ffn_w_down_proj):

    def _L0_attn_ref(x, WQ, bQ, WK, bK, WV, bV, proj):
        import jax, jax.numpy as jnp
        import numpy as np
        B, T, D = (4, 256, 256)
        HS, NH, NG = (128, 16, 4)
        R = NH // NG
        b, t, _ = x.shape
        Q = x @ WQ.T + bQ
        K = (x @ WK.T + bK).reshape(b, t, NG, HS)
        V = (x @ WV.T + bV).reshape(b, t, NG, HS)
        K = jnp.tile(K, (1, 1, R, 1)).reshape(b, t, NH * HS)
        V = jnp.tile(V, (1, 1, R, 1)).reshape(b, t, NH * HS)
        scores = jnp.einsum('btd,bsd->bts', Q, K)
        causal = jnp.triu(jnp.ones((t, t), dtype=bool), 1)
        scores = jnp.where(causal[None], -jnp.inf, scores)
        attn = jax.nn.softmax(scores, axis=-1) / jnp.sqrt(jnp.float32(HS))
        Z = jnp.einsum('bts,bsd->btd', attn, V)
        return Z @ proj

    def _L0_ffn_ref(x, w_gate_router, w_gate_proj, w_up_proj, w_down_proj):
        import jax, jax.numpy as jnp
        import numpy as np
        TOP_K = 2

        def moe_forward(x, w_gate_router, w_gate_proj, w_up_proj, w_down_proj):
            E = w_gate_router.shape[0]
            scores = jnp.einsum('bsd,ed->bse', x, w_gate_router)
            topk_scores, topk_idx = jax.lax.top_k(scores, TOP_K)
            topk_probs = jax.nn.softmax(topk_scores, axis=-1)
            weights = jnp.sum(topk_probs[..., None] * jax.nn.one_hot(topk_idx, E, dtype=x.dtype), axis=-2)
            gate = jnp.einsum('bsd,efd->bsef', x, w_gate_proj)
            up = jnp.einsum('bsd,efd->bsef', x, w_up_proj)
            hidden = jax.nn.silu(gate) * up
            out = jnp.einsum('bsef,edf,bse->bsd', hidden, w_down_proj, weights)
            return out
        return moe_forward(x, w_gate_router, w_gate_proj, w_up_proj, w_down_proj)
    x = L0_attn_x
    x = x + 0.5 * _L0_ffn_ref(_layernorm(x, axis=-1), L0_ffn_w_gate_router, L0_ffn_w_gate_proj, L0_ffn_w_up_proj, L0_ffn_w_down_proj)
    x = x + _L0_attn_ref(_layernorm(x, axis=-1), L0_attn_WQ, L0_attn_bQ, L0_attn_WK, L0_attn_bK, L0_attn_WV, L0_attn_bV, L0_attn_proj)
    x = x + 0.5 * _L0_ffn_ref(_layernorm(x, axis=-1), L0_ffn_w_gate_router, L0_ffn_w_gate_proj, L0_ffn_w_up_proj, L0_ffn_w_down_proj)
    return x

_drawn_inputs = setup_inputs


def setup_inputs(seed=0):
    import zlib

    import numpy as np

    out = dict(_drawn_inputs(seed))
    spreads = {}
    factors = {'L0_attn_bQ': 23.394, 'L0_attn_bK': 64.0, 'L0_attn_bV': 22.666}
    for name, (base, spread) in spreads.items():
        noise = np.random.default_rng([zlib.crc32(name.encode()), seed]).standard_normal(out[name].shape)
        drawn = base * np.exp(spread * noise) if base else spread * noise
        out[name] = jnp.asarray(drawn.astype(out[name].dtype))
    for name, factor in factors.items():
        out[name] = (out[name] * factor).astype(out[name].dtype)
    return out
```

```python
from contextlib import ExitStack

import numpy as np

import concourse.bass as bass
from concourse import mybir

F32 = mybir.dt.float32
F32R = mybir.dt.float32r
BF16 = mybir.dt.bfloat16
U32 = mybir.dt.uint32
ALU = mybir.AluOpType
ACT = mybir.ActivationFunctionType
AX = mybir.AxisListType

P = 128
B, T, D = 4, 1024, 256
KD = D // P
TILES = B * T // P
E, FE = 8, 96
F = E * FE
FB = F // P
CT = 4
CN = CT * P
CHUNKS = TILES // CT
HS, NH, NG = 128, 16, 4
R = NH // NG
QT = T // P
EPS = 1e-5
MASKED = -3.0e38


def need(eng, sem, value):
    if isinstance(value, int) and value <= 0:
        return
    eng.wait_ge(sem, value)


class Chain:

    def __init__(self, nc, eng, sem, base, spare):
        self.nc, self.eng, self.sem, self.base, self.spare, self.n = nc, eng, sem, base, spare, 0

    def link(self, ins):
        self.n += 1
        ins.then_inc(self.sem, 1)

    def settle(self):
        self.eng.wait_ge(self.sem, self.base + self.n)

    def settle_first(self):
        self.settle()
        self.nc.vector.memset(self.spare, 0.0)


def split_terms(hi_a, lo_a, hi_b, lo_b):
    return [(hi_a, hi_b), (hi_a, lo_b), (lo_a, hi_b)]


def as_f32(ap):
    return ap.bitcast(F32)


def moe_phase(nc, name, x, consts, w, load=None, store=None):
    ident, sel, pair, iota = consts["ident"], consts["sel"], consts["pair"], consts["iota"]
    VSTEPS = 16
    with ExitStack() as ctx:
        def sb(n, shape, dt=F32):
            return ctx.enter_context(nc.sbuf_tensor(f"{name}_{n}", shape, dt))

        def ps(n, shape):
            return ctx.enter_context(nc.psum_tensor(f"{name}_{n}", shape, F32))

        def sem(n):
            return ctx.enter_context(nc.semaphore(f"{name}_{n}"))

        stats = sb("stats", [P, CT, 6])
        mv = sb("mv", [P, CT, 2])
        veps = sb("veps", [P, CT])
        rstd = sb("rstd", [P, CT])
        xn = sb("xn", [P, CT, D])
        xt_hi = sb("xt_hi", [P, 2, KD, CN], F32R)
        xt_lo = sb("xt_lo", [P, 2, KD, CN], F32R)
        lg_t = sb("lg_t", [2 * E, CN])
        lg = sb("lg", [P, CT, E])
        top = sb("top", [P, CT, 8])
        top_i = sb("top_i", [P, CT, 8], U32)
        top_f = sb("top_f", [P, CT, 2])
        gap = sb("gap", [P, CT])
        th = sb("th", [P, CT])
        spare = sb("spare", [P, 1])
        prob = sb("prob", [P, CT, 2])
        one1 = sb("one1", [P, CT, E])
        one2 = sb("one2", [P, CT, E])
        wtok = sb("wtok", [P, CT, E])
        wsp = sb("wsp", [P, CT, 2, E], F32R)
        wt = sb("wt", [2 * E, 2, CN], F32R)
        sg = sb("sg", [P, 2, CN])
        gu = sb("gu", [P, 2, CN])
        hid = sb("hid", [P, 2, CN])
        h_hi = sb("h_hi", [P, 2, FB, CN], F32R)
        h_lo = sb("h_lo", [P, 2, FB, CN], F32R)

        gate_ps = [ps(f"gate{i}", [P, CN]) for i in range(2)]
        up_ps = [ps(f"up{i}", [P, CN]) for i in range(2)]
        wb_ps = ps("wb", [P, CN])
        dn_ps = [ps(f"dn{i}", [P, CN]) for i in range(2)]
        misc_ps = ps("misc", [P, CN])

        stats_done, rstd_done, xn_done = sem("stats_done"), sem("rstd_done"), sem("xn_done")
        xt_made, xt_hi_done, xt_lo_done = sem("xt_made"), sem("xt_hi_done"), sem("xt_lo_done")
        lg_made, lg_t_done, lg_tok_made = sem("lg_made"), sem("lg_t_done"), sem("lg_tok_made")
        gap_done, th_done, wsp_done = sem("gap_done"), sem("th_done"), sem("wsp_done")
        wt_made, wt_done = sem("wt_made"), sem("wt_done")
        gate_made, up_made, wb_made = sem("gate_made"), sem("up_made"), sem("wb_made")
        silu_done, gu_done, hid_done = sem("silu_done"), sem("gu_done"), sem("hid_done")
        hi_done, lo_done = sem("hi_done"), sem("lo_done")
        dn_made, dn_free = sem("dn_made"), sem("dn_free")
        vstep, pstep = sem("vstep"), sem("pstep")

        block = ctx.enter_context(nc.Block())

        if load is not None:
            raw_gu = sb("raw_gu", [P, KD, 2 * F])
            raw_dn = sb("raw_dn", [P, FB, D])
            raw_rt = sb("raw_rt", [P, KD, E])
            raw_sel = sb("raw_sel", [2 * E, FB, P])
            x_in, gu_in, dn_in, small_in = sem("x_in"), sem("gu_in"), sem("dn_in"), sem("small_in")
            id_in, wsplit = sem("id_in"), sem("wsplit")
            att_in, folded, rep_in = sem("att_in"), sem("folded"), [sem("wq_rep_in"), sem("proj_rep_in")]
            repeats = [raw_gu[:, :, :].rearrange("p k n -> p (k n)")[:, r * NG * D:(r + 1) * NG * D] for r in range(R - 1)]
            GU_READY, RT_READY, DN_READY = 2, 5, 7

        if load is not None or store is not None:
            @block.sync
            def _(sp):
                if load is not None:
                    sp.dma_start(ident[:, :], load["ident"]).then_inc(id_in, 16)
                    for c in range(CHUNKS):
                        sp.dma_start(x[:, c * CT:(c + 1) * CT, :], load["x"][:, c * CT:(c + 1) * CT, :]).then_inc(x_in, 16)
                        sp.wait_ge(x_in, 16 * (c + 1))
                    for n in ("ident_b", "mask_b"):
                        sp.dma_start(consts[n][:, :], load[n]).then_inc(att_in, 16)
                    for n in ("wq", "wk", "wv", "proj", "bq", "bk", "bv"):
                        sp.dma_start(load["attn"][n][0], load["attn"][n][1]).then_inc(att_in, 16)
                    sp.wait_ge(wsplit, GU_READY)
                    for i, n in enumerate(("wq", "proj")):
                        if i:
                            sp.wait_ge(folded, R - 1)
                        for r in range(1, R):
                            sp.dma_start(repeats[r - 1], load["attn"][n + "_repeats"][r]).then_inc(rep_in[i], 16)
                if store is not None:
                    for c in range(CHUNKS):
                        sp.wait_ge(dn_free, CT * (c + 1) + 2)
                        sp.dma_start(store["out"][:, c * CT:(c + 1) * CT, :],
                                     x[:, c * CT:(c + 1) * CT, :]).then_inc(store["sem"], 16)
                    sp.wait_ge(store["sem"], 16 * CHUNKS)

        @block.gpsimd
        def _(pool):
            def rstd_of(c):
                pool.wait_ge(stats_done, c + 1)
                nc.gpsimd.tensor_tensor(veps[:, :], mv[:, :, 1], consts["eps"][:, :], ALU.add).then_inc(pstep, 1)
                pool.wait_ge(pstep, c + 1)
                nc.gpsimd.tensor_tensor(rstd[:, :], veps[:, :], consts["mhalf"][:, :], ALU.pow).then_inc(rstd_done, 1)
            if load is not None:
                pool.wait_ge(small_in, 16 * 6)
            rstd_of(0)
            with pool.Fori(1, CHUNKS) as c:
                rstd_of(c)
            if load is not None:
                pool.wait_ge(att_in, 16 * 9)
                for i, total in enumerate((load["attn"]["wq"][0], load["attn"]["proj"][0])):
                    flat = total.rearrange("p g d -> p (g d)")
                    pool.wait_ge(rep_in[i], 16 * (R - 1))
                    for r in range(R - 1):
                        nc.gpsimd.tensor_tensor(flat, flat, repeats[r], ALU.add).then_inc(folded, 1)
                        pool.wait_ge(folded, i * (R - 1) + r + 1)
                bq = load["attn"]["bq"][0]
                for r in range(1, R):
                    nc.gpsimd.tensor_tensor(bq[:, 0, :], bq[:, 0, :], bq[:, r, :], ALU.add).then_inc(folded, 1)
                    pool.wait_ge(folded, 2 * (R - 1) + r)

        @block.scalar
        def _(act):
            if load is not None:
                for k in range(KD):
                    act.dma_start(raw_gu[:, k, 0:F], load["w_gate"][:, k, :]).then_inc(gu_in, 16)
                    act.dma_start(raw_gu[:, k, F:2 * F], load["w_up"][:, k, :]).then_inc(gu_in, 16)
                act.dma_start(raw_rt[:, :, :], load["w_router"]).then_inc(small_in, 16)
                act.dma_start(raw_sel[:, :, :], load["sel"]).then_inc(small_in, 16)
                act.dma_start(pair[:, :], load["pair"]).then_inc(small_in, 16)
                act.dma_start(iota[:, :], load["iota"]).then_inc(small_in, 16)
                act.dma_start(consts["eps"][:, :], load["eps"]).then_inc(small_in, 16)
                act.dma_start(consts["mhalf"][:, :], load["mhalf"]).then_inc(small_in, 16)
                act.dma_start(raw_dn[:, :, :], load["w_down"]).then_inc(dn_in, 16)

            def silu(c, fb):
                n = c * FB + fb
                act.wait_ge(gate_made, n + 1)
                need(act, gu_done, n - 1)
                nc.scalar.activation(sg[:, fb % 2, :], gate_ps[fb % 2][:, :], ACT.Silu).then_inc(silu_done, 1)

            def hi(c, par, fb):
                act.wait_ge(hid_done, c * FB + fb + 1)
                nc.scalar.activation(h_hi[:, par, fb, :], hid[:, fb % 2, :], ACT.Copy).then_inc(hi_done, 1)

            def xt_high(c, par, k):
                act.wait_ge(xt_made, KD * c + k + 1)
                nc.scalar.activation(xt_hi[:, par, k, :], misc_ps[:, :], ACT.Copy).then_inc(xt_hi_done, 1)

            def logits_out(c):
                act.wait_ge(lg_made, c + 1)
                nc.scalar.activation(lg_t[:, :], misc_ps[0:2 * E, :], ACT.Copy).then_inc(lg_t_done, 1)

            def tanh(c):
                act.wait_ge(gap_done, c + 1)
                nc.scalar.activation(th[:, :], gap[:, :], ACT.Tanh, scale=0.5).then_inc(th_done, 1)

            def weights_out(c, par):
                act.wait_ge(wt_made, c + 1)
                nc.scalar.activation(wt[:, par, :], misc_ps[0:2 * E, :], ACT.Copy).then_inc(wt_done, 1)

            def chunk(c, par, last):
                silu(c, 0)
                silu(c, 1)
                hi(c, par, 0)
                hi(c, par, 1)
                if not last:
                    xt_high(c + 1, 1 - par, 0)
                    xt_high(c + 1, 1 - par, 1)
                silu(c, 2)
                if not last:
                    logits_out(c + 1)
                hi(c, par, 2)
                silu(c, 3)
                hi(c, par, 3)
                silu(c, 4)
                if not last:
                    tanh(c + 1)
                hi(c, par, 4)
                silu(c, 5)
                if not last:
                    weights_out(c + 1, 1 - par)
                hi(c, par, 5)

            xt_high(0, 0, 0)
            xt_high(0, 0, 1)
            logits_out(0)
            tanh(0)
            weights_out(0, 0)
            chunk(0, 0, False)
            with act.Fori(0, (CHUNKS - 2) // 2) as j:
                chunk(2 * j + 1, 1, False)
                chunk(2 * j + 2, 0, False)
            chunk(CHUNKS - 1, 1, True)

        @block.vector
        def _(dve):
            if load is not None:
                def split(src, dst_hi, dst_lo, count):
                    nc.vector.tensor_copy(dst_hi, src).then_inc(wsplit, 1)
                    dve.wait_ge(wsplit, count + 1)
                    nc.vector.tensor_tensor(dst_lo, src, as_f32(dst_hi), ALU.subtract).then_inc(wsplit, 1)

            def statistics(c):
                if load is not None:
                    dve.wait_ge( x_in, 16 * (c + 1))
                chain = Chain(nc, dve, vstep, VSTEPS * c, spare[:, :])
                for k in range(CT):
                    chain.link(nc.vector.bn_stats(stats[:, k, :], x[:, c * CT + k, :]))
                chain.settle_first()
                for k in range(CT):
                    last = nc.vector.bn_aggr(mv[:, k, :], stats[:, k, :])
                last.then_inc(stats_done, 1)

            def normalise(c):
                dve.wait_ge(rstd_done, c + 1)
                need(dve, xt_made, KD * c)
                for k in range(CT):
                    last = nc.vector.tensor_scalar(xn[:, k, :], x[:, c * CT + k, :], mv[:, k, 0:1], rstd[:, k:k + 1],
                                                   ALU.subtract, ALU.mult)
                last.then_inc(xn_done, 1)

            def xt_low(c, par, k):
                dve.wait_ge(xt_hi_done, KD * c + k + 1)
                nc.vector.tensor_tensor(xt_lo[:, par, k, :], misc_ps[:, :], as_f32(xt_hi[:, par, k, :]),
                                        ALU.subtract).then_inc(xt_lo_done, 1)

            def top_two(c):
                chain = Chain(nc, dve, vstep, VSTEPS * c + CT, spare[:, :])
                dve.wait_ge(lg_tok_made, c + 1)
                chain.link(nc.vector.tensor_copy(lg[:, :, :], misc_ps[:, 0:CT * E].rearrange("p (k e) -> p k e", e=E)))
                chain.settle_first()
                for k in range(CT):
                    chain.link(nc.vector.max(top[:, k, :], lg[:, k, :]))
                chain.settle()
                nc.vector.tensor_tensor(gap[:, :], top[:, :, 0], top[:, :, 1], ALU.subtract).then_inc(gap_done, 1)
                for k in range(CT):
                    last = nc.vector.max_index(top_i[:, k, :], top[:, k, :], lg[:, k, :])
                chain.link(last)
                chain.settle()
                chain.link(nc.vector.tensor_copy(top_f[:, :, :], top_i[:, :, 0:2]))
                chain.settle()
                i8 = iota[:, :].rearrange("p (k e) -> p k e", e=E)
                for r, one in enumerate((one1, one2)):
                    last = nc.vector.tensor_tensor(one[:, :, :], i8, top_f[:, :, r:r + 1].broadcast_to([P, CT, E]),
                                                   ALU.is_equal)
                chain.link(last)
                assert chain.n == 8, chain.n

            def token_weights(c):
                chain = Chain(nc, dve, vstep, VSTEPS * c + CT + 8, spare[:, :])
                dve.wait_ge(th_done, c + 1)
                nc.vector.tensor_scalar(prob[:, :, 0], th[:, :], 0.25, 0.25, ALU.mult, ALU.add)
                chain.link(nc.vector.tensor_scalar(prob[:, :, 1], th[:, :], -0.25, 0.25, ALU.mult, ALU.add))
                chain.settle()
                nc.vector.tensor_tensor(one1[:, :, :], one1[:, :, :], prob[:, :, 0:1].broadcast_to([P, CT, E]), ALU.mult)
                chain.link(nc.vector.tensor_tensor(one2[:, :, :], one2[:, :, :],
                                                   prob[:, :, 1:2].broadcast_to([P, CT, E]), ALU.mult))
                chain.settle()
                chain.link(nc.vector.tensor_tensor(wtok[:, :, :], one1[:, :, :], one2[:, :, :], ALU.add))
                chain.settle()
                chain.link(nc.vector.tensor_copy(wsp[:, :, 0, :], wtok[:, :, :]))
                chain.settle()
                nc.vector.tensor_tensor(wsp[:, :, 1, :], wtok[:, :, :], as_f32(wsp[:, :, 0, :]),
                                        ALU.subtract).then_inc(wsp_done, 1)

            def gate_up(c, fb):
                n = c * FB + fb
                dve.wait_ge(silu_done, n + 1)
                dve.wait_ge(up_made, n + 1)
                nc.vector.tensor_tensor(gu[:, fb % 2, :], sg[:, fb % 2, :], up_ps[fb % 2][:, :], ALU.mult).then_inc(gu_done, 1)

            def weigh(c, fb):
                n = c * FB + fb
                dve.wait_ge(wb_made, n + 1)
                dve.wait_ge(gu_done, n + 1)
                nc.vector.tensor_tensor(hid[:, fb % 2, :], gu[:, fb % 2, :], wb_ps[:, :], ALU.mult).then_inc(hid_done, 1)

            def low(c, par, fb):
                n = c * FB + fb
                dve.wait_ge(hi_done, n + 1)
                nc.vector.tensor_tensor(h_lo[:, par, fb, :], hid[:, fb % 2, :], as_f32(h_hi[:, par, fb, :]),
                                        ALU.subtract).then_inc(lo_done, 1)

            def residual(c, k):
                dve.wait_ge(dn_made, CT * c + k + 1)
                nc.vector.tensor_tensor(x[:, c * CT + k, :], dn_ps[k % 2][:, 0:D], x[:, c * CT + k, :],
                                        ALU.add).then_inc(dn_free, 1)

            def chunk(c, par, first, last):
                if not last:
                    statistics(c + 1)
                gate_up(c, 0)
                if not first:
                    low(c - 1, 1 - par, FB - 1)
                weigh(c, 0)
                gate_up(c, 1)
                low(c, par, 0)
                weigh(c, 1)
                if not last:
                    normalise(c + 1)
                low(c, par, 1)
                for k in range(CT):
                    if not first:
                        residual(c - 1, k)
                    if not last and k < KD:
                        xt_low(c + 1, 1 - par, k)
                gate_up(c, 2)
                weigh(c, 2)
                gate_up(c, 3)
                low(c, par, 2)
                weigh(c, 3)
                if not last:
                    top_two(c + 1)
                gate_up(c, 4)
                low(c, par, 3)
                weigh(c, 4)
                if not last:
                    token_weights(c + 1)
                gate_up(c, 5)
                low(c, par, 4)
                weigh(c, 5)

            nc.vector.memset(gap[:, :], 0.0).then_inc(dn_free, 2)
            statistics(0)
            if load is not None:
                dve.wait_ge(gu_in, 16 * 2 * KD)
                split(raw_gu[:, :, :], w["gu_hi"][:, :, :], w["gu_lo"][:, :, :], 0)
            normalise(0)
            if load is not None:
                dve.wait_ge(small_in, 16 * 6)
                split(raw_rt[:, :, :], w["rt"][:, :, 0:E], w["rt"][:, :, E:2 * E], 2)
                nc.vector.tensor_copy(sel[:, :, :], raw_sel[:, :, :]).then_inc(wsplit, 1)
            xt_low(0, 0, 0)
            xt_low(0, 0, 1)
            top_two(0)
            token_weights(0)
            if load is not None:
                dve.wait_ge(dn_in, 16)
                split(raw_dn[:, :, :], w["dn_hi"][:, :, :], w["dn_lo"][:, :, :], 5)
            chunk(0, 0, True, False)
            with dve.Fori(0, (CHUNKS - 2) // 2) as j:
                chunk(2 * j + 1, 1, False, False)
                chunk(2 * j + 2, 0, False, False)
            chunk(CHUNKS - 1, 1, False, True)
            low(CHUNKS - 1, 1, FB - 1)
            for k in range(CT):
                residual(CHUNKS - 1, k)

        @block.tensor
        def _(pe):
            def transposes(c, k):
                pe.wait_ge(xn_done, c + 1)
                if k > 0:
                    pe.wait_ge(xt_lo_done, KD * c + k)
                for t in range(CT):
                    last = nc.tensor.transpose(misc_ps[:, t * P:(t + 1) * P], xn[:, t, k * P:(k + 1) * P], ident[:, :])
                last.then_inc(xt_made, 1)

            def logits(c, par):
                pe.wait_ge(xt_lo_done, KD * (c + 1))
                terms = [(k, xt) for xt in (xt_hi, xt_lo) for k in range(KD)]
                for i, (k, xt) in enumerate(terms):
                    last = nc.tensor.matmul(misc_ps[0:2 * E, :], w["rt"][:, k, :], xt[:, par, k, :],
                                            start=i == 0, stop=i == len(terms) - 1)
                last.then_inc(lg_made, 1)

            def logits_by_token(c):
                pe.wait_ge(lg_t_done, c + 1)
                for t in range(CT):
                    last = nc.tensor.matmul(misc_ps[:, t * E:(t + 1) * E], lg_t[:, t * P:(t + 1) * P], pair[:, :],
                                            start=True, stop=True)
                last.then_inc(lg_tok_made, 1)

            def weights_by_feature(c):
                pe.wait_ge(wsp_done, c + 1)
                for t in range(CT):
                    last = nc.tensor.transpose(misc_ps[0:2 * E, t * P:(t + 1) * P],
                                               as_f32(wsp[:, t, :, :]).rearrange("p a e -> p (a e)"), ident[:, :])
                last.then_inc(wt_made, 1)

            def product(out, block_of, par):
                terms = [(k, a, b) for a, b in split_terms("gu_hi", "gu_lo", xt_hi, xt_lo) for k in range(KD)]
                for i, (k, a, b) in enumerate(terms):
                    last = nc.tensor.matmul(out, w[a][:, k, block_of], b[:, par, k, :],
                                            start=i == 0, stop=i == len(terms) - 1)
                return last

            def gate(c, par, fb):
                need(pe, silu_done, c * FB + fb - 1)
                product(gate_ps[fb % 2][:, :], slice(fb * P, (fb + 1) * P), par).then_inc(gate_made, 1)

            def up(c, par, fb):
                need(pe, gu_done, c * FB + fb - 1)
                product(up_ps[fb % 2][:, :], slice(F + fb * P, F + (fb + 1) * P), par).then_inc(up_made, 1)

            def weight(c, par, fb):
                need(pe, hid_done, c * FB + fb)
                if fb == 0:
                    pe.wait_ge(wt_done, c + 1)
                nc.tensor.matmul(wb_ps[:, :], sel[:, fb, :], wt[:, par, :], start=True, stop=True).then_inc(wb_made, 1)

            def down(c, par, t):
                if t == 0:
                    pe.wait_ge(lo_done, FB * (c + 1))
                    if load is not None and isinstance(c, int) and c == 0:
                        pe.wait_ge(wsplit, DN_READY)
                pe.wait_ge(dn_free, CT * c + t + 1)
                terms = [(fb, a, b) for fb in range(FB) for a, b in split_terms(h_hi, h_lo, "dn_hi", "dn_lo")]
                for i, (fb, a, b) in enumerate(terms):
                    last = nc.tensor.matmul(dn_ps[t % 2][:, 0:D], a[:, par, fb, t * P:(t + 1) * P], w[b][:, fb, :],
                                            start=i == 0, stop=i == len(terms) - 1)
                last.then_inc(dn_made, 1)

            def hidden(c, par, fb):
                gate(c, par, fb)
                up(c, par, fb)
                weight(c, par, fb)

            def chunk(c, par, first, last):
                hidden(c, par, 0)
                hidden(c, par, 1)
                for t in range(CT):
                    if not first:
                        down(c - 1, 1 - par, t)
                    if not last and t < KD:
                        transposes(c + 1, t)
                hidden(c, par, 2)
                if not last:
                    logits(c + 1, 1 - par)
                hidden(c, par, 3)
                if not last:
                    logits_by_token(c + 1)
                hidden(c, par, 4)
                gate(c, par, 5)
                up(c, par, 5)
                if not last:
                    weights_by_feature(c + 1)
                weight(c, par, 5)

            if load is not None:
                pe.wait_ge(id_in, 16)
            transposes(0, 0)
            transposes(0, 1)
            if load is not None:
                pe.wait_ge(wsplit, RT_READY)
                pe.wait_ge(small_in, 16 * 6)
            logits(0, 0)
            logits_by_token(0)
            weights_by_feature(0)
            chunk(0, 0, True, False)
            with pe.Fori(0, (CHUNKS - 2) // 2) as j:
                chunk(2 * j + 1, 1, False, False)
                chunk(2 * j + 2, 0, False, False)
            chunk(CHUNKS - 1, 1, False, True)
            for t in range(CT):
                down(CHUNKS - 1, 1, t)


def attention_phase(nc, x, consts, aw):
    ident = consts["ident"]
    STEPS = B * QT
    VW = D + 2
    groups = [(i + CT) // CT for i in range(QT)]
    GROUPS = sum(groups)

    def group0(g):
        return g // QT * GROUPS + sum(groups[:g % QT])

    order = [("t", t) for t in range(QT)] + [("y", 0, 0, m) for m in range(KD)] + [("v", t) for t in range(QT - 1)]
    at_step = []
    for g in range(STEPS):
        b, i = divmod(g, QT)
        t_unit = ("t", g + QT) if b + 1 < B else None
        v_unit = ("v", g + QT - 1) if g + QT - 1 < B * QT else None
        y_unit = ("y", b, 1, i) if i < KD else ("y", b + 1, 0, i - 5) if 5 <= i < 5 + KD and b + 1 < B else None
        at_step.append((t_unit, v_unit, y_unit))
        order += [u for u in (t_unit, v_unit, y_unit) if u]
    unit = {u: n for n, u in enumerate(order)}
    high = {u: n for n, u in enumerate(u for u in order if u[0] != "v")}

    with ExitStack() as ctx:
        def sb(n, shape, dt=F32):
            return ctx.enter_context(nc.sbuf_tensor(f"att_{n}", shape, dt))

        def ps(n, shape):
            return ctx.enter_context(nc.psum_tensor(f"att_{n}", shape, F32))

        def sem(n):
            return ctx.enter_context(nc.semaphore(f"att_{n}"))

        a_hi, a_lo = sb("a_hi", [P, KD, D], F32R), sb("a_lo", [P, KD, D], F32R)
        b_hi, b_lo, b_f = sb("b_hi", [P, KD, VW], F32R), sb("b_lo", [P, KD, VW], F32R), sb("b_f", [P, KD, VW])
        y_bias, v_bias = sb("y_bias", [P, KD]), sb("v_bias", [P, VW])
        stats, mv = sb("stats", [P, 2, 6]), sb("mv", [P, 2, 2])
        veps, rstd = sb("veps", [P, 2]), sb("rstd", [P, 2])
        xn = sb("xn", [P, 2, D])
        xt_hi, xt_lo = sb("xt_hi", [P, 2, KD, T], F32R), sb("xt_lo", [P, 2, KD, T], F32R)
        yt_hi, yt_lo = sb("yt_hi", [P, KD, T], F32R), sb("yt_lo", [P, KD, T], F32R)
        v_f = sb("v_f", [P, 2, D])
        v_hi, v_lo = sb("v_hi", [P, 2, QT, D], F32R), sb("v_lo", [P, 2, QT, D], F32R)
        shift = sb("shift", [P, 2, QT])
        neg_max, bias = sb("neg_max", [P, 2]), sb("bias", [P, 2])
        prob = sb("prob", [P, 2, T])
        total, inv = sb("total", [P, 2]), sb("inv", [P, 2])
        pt_hi, pt_lo = sb("pt_hi", [P, QT, P], F32R), sb("pt_lo", [P, QT, P], F32R)

        s_ps = [ps(f"s{i}", [P, T]) for i in range(2)]
        pt_ps = [ps(f"pt{i}", [P, CT * P]) for i in range(2)]
        pv_ps, misc_ps = ps("pv", [P, CT * P]), ps("misc", [P, CT * P])

        folded, split_done, b_scaled = sem("folded"), sem("split_done"), sem("b_scaled")
        stats_made, stats_done, rstd_done, xn_done = (sem(n) for n in ("stats_made", "stats_done", "rstd_done", "xn_done"))
        pstep = sem("pstep")
        misc_made, misc_hi, misc_free = sem("misc_made"), sem("misc_hi"), sem("misc_free")
        shift_done, v_hi_done, v_done = sem("shift_done"), sem("v_hi_done"), sem("v_done")
        s_made, max_done, bias_done, exp_done = sem("s_made"), sem("max_done"), sem("bias_done"), sem("exp_done")
        pt_made, pt_hi_done, pt_lo_done = sem("pt_made"), sem("pt_hi_done"), sem("pt_lo_done")
        inv_done, pv_made, x_done = sem("inv_done"), sem("pv_made"), sem("x_done")

        block = ctx.enter_context(nc.Block())

        @block.gpsimd
        def _(pool):
            for t in range(B * QT):
                pool.wait_ge(stats_done, t + 1)
                need(pool, xn_done, t - 1)
                nc.gpsimd.tensor_tensor(veps[:, t % 2:t % 2 + 1], mv[:, t % 2, 1:2], consts["eps"][:, 0:1],
                                        ALU.add).then_inc(pstep, 1)
                pool.wait_ge(pstep, t + 1)
                nc.gpsimd.tensor_tensor(rstd[:, t % 2:t % 2 + 1], veps[:, t % 2:t % 2 + 1], consts["mhalf"][:, 0:1],
                                        ALU.pow).then_inc(rstd_done, 1)

        @block.scalar
        def _(act):
            def xt_high(t):
                b, i = divmod(t, QT)
                act.wait_ge(misc_made, unit[("t", t)] + 1)
                nc.scalar.activation(xt_hi[:, b % 2, :, i * P:(i + 1) * P],
                                     misc_ps[:, 0:D].rearrange("p (k c) -> p k c", k=KD), ACT.Copy).then_inc(misc_hi, 1)

            def y_high(b, h, m):
                act.wait_ge(misc_made, unit[("y", b, h, m)] + 1)
                nc.scalar.activation(yt_hi[:, m, h * CN:(h + 1) * CN], misc_ps[:, :], ACT.Identity,
                                     bias=y_bias[:, m:m + 1]).then_inc(misc_hi, 1)

            def v_high(t):
                b, i = divmod(t, QT)
                act.wait_ge(misc_free, unit[("v", t)] + 1)
                nc.scalar.activation(v_hi[:, b % 2, i, :], v_f[:, t % 2, :], ACT.Copy).then_inc(v_hi_done, 1)

            def exps(g):
                n = (g % QT + 1) * P
                act.wait_ge(bias_done, g + 1)
                need(act, inv_done, g - 1)
                nc.scalar.activation(prob[:, g % 2, 0:n], s_ps[g % 2][:, 0:n], ACT.Exp, bias=bias[:, g % 2:g % 2 + 1],
                                     accum_out=total[:, g % 2:g % 2 + 1]).then_inc(exp_done, 1)

            def pt_high(g, r):
                n = min(CT, g % QT + 1 - r * CT) * P
                G = group0(g) + r
                act.wait_ge(pt_made, G + 1)
                out = pt_hi[:, r * CT:r * CT + n // P, :].rearrange("p k c -> p (k c)")
                nc.scalar.activation(out, pt_ps[G % 2][:, 0:n], ACT.Copy).then_inc(pt_hi_done, 1)

            act.wait_ge(split_done, 1)
            for u in order[:unit[("v", QT - 2)] + 1]:
                {"t": xt_high, "y": y_high, "v": v_high}[u[0]](*u[1:])
            for g in range(STEPS + 1):
                t_unit, v_unit, y_unit = at_step[g] if g < STEPS else (None,) * 3
                if t_unit:
                    xt_high(*t_unit[1:])
                if g > 0:
                    pt_high(g - 1, 0)
                if v_unit:
                    v_high(*v_unit[1:])
                if g > 0 and groups[(g - 1) % QT] > 1:
                    pt_high(g - 1, 1)
                if g < STEPS:
                    exps(g)
                if y_unit:
                    y_high(*y_unit[1:])

        @block.vector
        def _(dve):
            def statistics(t):
                need(dve, rstd_done, t - 1)
                nc.vector.bn_stats(stats[:, t % 2, :], x[:, t, :]).then_inc(stats_made, 1)
                dve.wait_ge(stats_made, t + 1)
                nc.vector.bn_aggr(mv[:, t % 2, :], stats[:, t % 2, :]).then_inc(stats_done, 1)

            def normalise(t):
                dve.wait_ge(rstd_done, t + 1)
                if t >= 2:
                    dve.wait_ge(misc_made, unit[("t", t - 2)] + 1)
                nc.vector.tensor_scalar(xn[:, t % 2, :], x[:, t, :], mv[:, t % 2, 0:1], rstd[:, t % 2:t % 2 + 1],
                                        ALU.subtract, ALU.mult).then_inc(xn_done, 1)

            def xt_low(t):
                b, i = divmod(t, QT)
                cols = slice(i * P, (i + 1) * P)
                dve.wait_ge(misc_hi, high[("t", t)] + 1)
                nc.vector.tensor_tensor(xt_lo[:, b % 2, :, cols], misc_ps[:, 0:D].rearrange("p (k c) -> p k c", k=KD),
                                        as_f32(xt_hi[:, b % 2, :, cols]), ALU.subtract).then_inc(misc_free, 1)

            def y_low(b, h, m):
                cols = slice(h * CN, (h + 1) * CN)
                dve.wait_ge(misc_hi, high[("y", b, h, m)] + 1)
                nc.vector.scalar_tensor_tensor(yt_lo[:, m, cols], misc_ps[:, :], y_bias[:, m:m + 1],
                                               as_f32(yt_hi[:, m, cols]), ALU.add, ALU.subtract).then_inc(misc_free, 1)

            def v_value(t):
                b, i = divmod(t, QT)
                dve.wait_ge(misc_made, unit[("v", t)] + 1)
                need(dve, v_done, t - 1)
                nc.vector.tensor_tensor(shift[:, b % 2, i:i + 1], misc_ps[:, D:D + 1], v_bias[:, D:D + 1],
                                        ALU.add).then_inc(shift_done, 1)
                nc.vector.tensor_tensor(v_f[:, t % 2, :], misc_ps[:, 0:D], v_bias[:, 0:D], ALU.add).then_inc(misc_free, 1)

            def v_low(t):
                b, i = divmod(t, QT)
                dve.wait_ge(v_hi_done, t + 1)
                nc.vector.tensor_tensor(v_lo[:, b % 2, i, :], v_f[:, t % 2, :], as_f32(v_hi[:, b % 2, i, :]),
                                        ALU.subtract).then_inc(v_done, 1)

            def maximum(g):
                b, i = divmod(g, QT)
                dve.wait_ge(s_made, g + 1)
                nc.vector.tensor_reduce(neg_max[:, g % 2:g % 2 + 1], s_ps[g % 2][:, 0:(i + 1) * P], AX.X, ALU.max,
                                        negate=True).then_inc(max_done, 1)

            def exp_bias(g):
                b, i = divmod(g, QT)
                dve.wait_ge(max_done, g + 1)
                dve.wait_ge(shift_done, g + 1)
                c = shift[:, b % 2, i:i + 1]
                nc.vector.tensor_scalar(bias[:, g % 2:g % 2 + 1], neg_max[:, g % 2:g % 2 + 1], c, c,
                                        ALU.subtract, ALU.add).then_inc(bias_done, 1)

            def pt_low(g, r):
                k = min(CT, g % QT + 1 - r * CT)
                G = group0(g) + r
                dve.wait_ge(pt_hi_done, G + 1)
                blocks = slice(r * CT, r * CT + k)
                nc.vector.tensor_tensor(pt_lo[:, blocks, :].rearrange("p k c -> p (k c)"), pt_ps[G % 2][:, 0:k * P],
                                        as_f32(pt_hi[:, blocks, :]).rearrange("p k c -> p (k c)"),
                                        ALU.subtract).then_inc(pt_lo_done, 1)

            def inverse(g):
                dve.wait_ge(exp_done, g + 1)
                nc.vector.reciprocal(inv[:, g % 2:g % 2 + 1], total[:, g % 2:g % 2 + 1]).then_inc(inv_done, 1)

            def residual(g):
                dve.wait_ge(pv_made, g + 1)
                dve.wait_ge(inv_done, g + 1)
                nc.vector.scalar_tensor_tensor(x[:, g, :], pv_ps[:, 0:D], inv[:, g % 2:g % 2 + 1], x[:, g, :],
                                               ALU.mult, ALU.add).then_inc(x_done, 1)

            dve.wait_ge(folded, 1)
            nc.vector.tensor_copy(y_bias[:, :], pt_ps[1][:, 0:KD]).then_inc(split_done, 1)
            nc.vector.tensor_scalar(v_bias[:, 0:D], pt_ps[0][:, 0:D], HS ** -0.5, None, ALU.mult)
            nc.vector.tensor_copy(v_bias[:, D:D + 1], pt_ps[0][:, D:D + 1])
            nc.vector.memset(b_f[:, :, D + 1:VW], 0.0)
            for m in range(KD):
                cols = slice(m * CN, m * CN + D)
                nc.vector.tensor_copy(a_hi[:, m, :], s_ps[0][:, cols]).then_inc(split_done, 1)
                nc.vector.tensor_scalar(b_f[:, m, 0:D], s_ps[1][:, cols], HS ** -0.5, None, ALU.mult)
                nc.vector.tensor_copy(b_f[:, m, D:D + 1], s_ps[1][:, m * CN + D:m * CN + D + 1]).then_inc(b_scaled, 1)
            dve.wait_ge(split_done, 1 + KD)
            for m in range(KD):
                nc.vector.tensor_tensor(a_lo[:, m, :], s_ps[0][:, m * CN:m * CN + D], as_f32(a_hi[:, m, :]),
                                        ALU.subtract).then_inc(split_done, 1)
            dve.wait_ge(b_scaled, KD)
            nc.vector.tensor_copy(b_hi[:, :, :], b_f[:, :, :]).then_inc(split_done, 1)
            dve.wait_ge(split_done, 2 + 2 * KD)
            nc.vector.tensor_tensor(b_lo[:, :, :], b_f[:, :, :], as_f32(b_hi[:, :, :]), ALU.subtract).then_inc(split_done, 1)

            statistics(0)
            for t in range(QT):
                statistics(t + 1)
                normalise(t)
                xt_low(t)
            for m in range(KD):
                y_low(0, 0, m)
            for t in range(QT - 1):
                v_value(t)
                if t > 0:
                    v_low(t - 1)
            v_low(QT - 2)
            normalise(QT)
            for g in range(STEPS + 1):
                t_unit, v_unit, y_unit = at_step[g] if g < STEPS else (None,) * 3
                ahead = g + QT + 1
                if ahead < B * QT:
                    statistics(ahead)
                if t_unit:
                    xt_low(*t_unit[1:])
                if v_unit:
                    v_value(*v_unit[1:])
                if g < STEPS:
                    maximum(g)
                    exp_bias(g)
                if g > 0:
                    inverse(g - 1)
                    for r in range(groups[(g - 1) % QT]):
                        pt_low(g - 1, r)
                if v_unit:
                    v_low(*v_unit[1:])
                if y_unit:
                    y_low(*y_unit[1:])
                if ahead < B * QT:
                    normalise(ahead)
                if g > 0:
                    residual(g - 1)

        @block.tensor
        def _(pe):
            def group(out, pairs):
                for n, (a, b) in enumerate(pairs):
                    last = nc.tensor.matmul(out, a, b, start=n == 0, stop=n == len(pairs) - 1)
                return last

            def fold():
                wq, wk, wv, proj, bq, bk, bv = (aw[n] for n in ("wq", "wk", "wv", "proj", "bq", "bk", "bv"))
                gs = range(NG)
                for m in range(KD):
                    d = slice(m * P, (m + 1) * P)
                    group(s_ps[0][:, m * CN:m * CN + D], [(wq[:, g, d], wk[:, g, :]) for g in gs])
                    group(s_ps[1][:, m * CN:m * CN + D], [(wv[:, g, d], proj[:, g, :]) for g in gs])
                    group(s_ps[1][:, m * CN + D:m * CN + D + 1], [(wq[:, g, d], bk[:, g:g + 1]) for g in gs])
                    group(pt_ps[1][:, m:m + 1], [(wk[:, g, d], bq[:, 0, g:g + 1]) for g in gs])
                group(pt_ps[0][:, 0:D], [(bv[:, g:g + 1].broadcast_to([P, P]), proj[:, g, :]) for g in gs])
                group(pt_ps[0][:, D:D + 1], [(bq[:, 0, g:g + 1].broadcast_to([P, P]), bk[:, g:g + 1])
                                             for g in gs]).then_inc(folded, 1)

            def transposes(t):
                need(pe, misc_free, unit[("t", t)])
                pe.wait_ge(xn_done, t + 1)
                for k in range(KD):
                    last = nc.tensor.transpose(misc_ps[:, k * P:(k + 1) * P], xn[:, t % 2, k * P:(k + 1) * P], ident[:, :])
                last.then_inc(misc_made, 1)

            def y(b, h, m):
                pe.wait_ge(misc_free, unit[("y", b, h, m)])
                pairs = [(a[:, k, m * P:(m + 1) * P], t[:, b % 2, k, h * CN:(h + 1) * CN])
                         for a, t in split_terms(a_hi, a_lo, xt_hi, xt_lo) for k in range(KD)]
                group(misc_ps[:, :], pairs).then_inc(misc_made, 1)

            def v(t):
                b, i = divmod(t, QT)
                pe.wait_ge(misc_free, unit[("v", t)])
                pairs = [(a[:, b % 2, k, i * P:(i + 1) * P], w[:, k, :])
                         for a, w in split_terms(xt_hi, xt_lo, b_hi, b_lo) for k in range(KD)]
                group(misc_ps[:, 0:VW], pairs).then_inc(misc_made, 1)

            def scores(g):
                b, i = divmod(g, QT)
                need(pe, exp_done, g - 1)
                pe.wait_ge(misc_free, unit[("y", b, i // CT, KD - 1)] + 1)
                n = (i + 1) * P
                here = slice(i * P, (i + 1) * P)
                for c0 in range(0, n, CN):
                    width = min(CN, max(n - c0, 2 * P))
                    pairs = [(a[:, k, here], t[:, b % 2, k, c0:c0 + width])
                             for a, t in split_terms(yt_hi, yt_lo, xt_hi, xt_lo) for k in range(KD)]
                    for m, (q, keys) in enumerate(pairs):
                        nc.tensor.matmul(s_ps[g % 2][:, c0:c0 + width], q, keys, start=m == 0, stop=False,
                                         skip_group_check=True)
                last = nc.tensor.matmul(s_ps[g % 2][:, n - P:n], consts["ident_b"][:, :], consts["mask_b"][:, :],
                                        start=False, stop=True, skip_group_check=True)
                last.then_inc(s_made, 1)

            def prob_transposes(g):
                i = g % QT
                pe.wait_ge(exp_done, g + 1)
                for r in range(groups[i]):
                    G = group0(g) + r
                    need(pe, pt_lo_done, G - 1)
                    for k in range(r * CT, min(i + 1, (r + 1) * CT)):
                        last = nc.tensor.transpose(pt_ps[G % 2][:, (k - r * CT) * P:(k - r * CT + 1) * P],
                                                   prob[:, g % 2, k * P:(k + 1) * P], ident[:, :])
                    last.then_inc(pt_made, 1)

            def values(g):
                b, i = divmod(g, QT)
                need(pe, x_done, g)
                pe.wait_ge(v_done, g + 1)
                pe.wait_ge(pt_lo_done, group0(g) + groups[i])
                pairs = [(p[:, k, :], w[:, b % 2, k, :])
                         for k in range(i + 1) for p, w in split_terms(pt_hi, pt_lo, v_hi, v_lo)]
                group(pv_ps[:, 0:D], pairs).then_inc(pv_made, 1)

            fold()
            for t in range(QT):
                transposes(t)
            pe.wait_ge(split_done, 3 + 2 * KD)
            for m in range(KD):
                y(0, 0, m)
            for t in range(QT - 1):
                v(t)
            for g in range(STEPS + 1):
                t_unit, v_unit, y_unit = at_step[g] if g < STEPS else (None,) * 3
                if t_unit:
                    transposes(*t_unit[1:])
                if g < STEPS:
                    scores(g)
                if v_unit:
                    v(*v_unit[1:])
                if g > 0:
                    prob_transposes(g - 1)
                if y_unit:
                    y(*y_unit[1:])
                if g > 0:
                    values(g - 1)


def build(nc, a, out):
    with ExitStack() as ctx:
        def sb(n, shape, dt=F32):
            return ctx.enter_context(nc.sbuf_tensor(n, shape, dt))
        x = sb("x", [P, TILES, D])
        consts = {
            "ident": sb("ident", [P, P]),
            "sel": sb("sel", [2 * E, FB, P], F32R),
            "pair": sb("pair", [2 * E, E]),
            "iota": sb("iota", [P, CT * E]),
            "mhalf": sb("mhalf", [P, CT]),
            "eps": sb("eps", [P, CT]),
            "ident_b": sb("ident_b", [P, P], BF16), "mask_b": sb("mask_b", [P, P], BF16),
        }
        w = {
            "gu_hi": sb("gu_hi", [P, KD, 2 * F], F32R), "gu_lo": sb("gu_lo", [P, KD, 2 * F], F32R),
            "dn_hi": sb("dn_hi", [P, FB, D], F32R), "dn_lo": sb("dn_lo", [P, FB, D], F32R),
            "rt": sb("rt", [P, KD, 2 * E], F32R),
        }
        aw = {
            "wq": sb("wq", [P, NG, D]), "wk": sb("wk", [P, NG, D]), "wv": sb("wv", [P, NG, D]),
            "proj": sb("proj", [P, NG, D]),
            "bq": sb("bq", [P, R, NG]), "bk": sb("bk", [P, NG]), "bv": sb("bv", [P, NG]),
        }
        repeats = {n: a[n].rearrange("(r g h) d -> r h g d", h=P, g=NG) for n in ("wq", "proj")}
        attn = {
            "wq": (aw["wq"][:, :, :], repeats["wq"][0]), "proj": (aw["proj"][:, :, :], repeats["proj"][0]),
            "wq_repeats": repeats["wq"], "proj_repeats": repeats["proj"],
            "wk": (aw["wk"][:, :, :], a["wk"].rearrange("(g h) d -> h g d", h=P)),
            "wv": (aw["wv"][:, :, :], a["wv"].rearrange("(g h) d -> h g d", h=P)),
            "bq": (aw["bq"][:, :, :], a["bq"]), "bk": (aw["bk"][:, :], a["bk"]), "bv": (aw["bv"][:, :], a["bv"]),
        }
        load = {
            "attn": attn,
            "x": a["x"].rearrange("b (n p) d -> p (b n) d", p=P),
            "w_gate": a["w_gate"].rearrange("(k p) f -> p k f", p=P),
            "w_up": a["w_up"].rearrange("(k p) f -> p k f", p=P),
            "w_down": a["w_down"].rearrange("(k p) f -> p k f", p=P),
            "w_router": a["w_router"].rearrange("(k p) e -> p k e", p=P),
            "sel": a["sel"], "pair": a["pair"], "iota": a["iota"], "mhalf": a["mhalf"], "eps": a["eps"], "ident": a["ident"],
            "ident_b": a["ident_b"], "mask_b": a["mask_b"],
        }
        moe_phase(nc, "moe1", x, consts, w, load=load)
        attention_phase(nc, x, consts, aw)
        out_t = out.rearrange("b (n p) d -> p (b n) d", p=P)
        stored = ctx.enter_context(nc.semaphore("stored"))
        moe_phase(nc, "moe2", x, consts, w, store={"out": out_t, "sem": stored})


def kernel(**inputs):
    import concourse.bacc as bacc
    from concourse.bass_utils import run_bass_kernel_spmd

    bf16 = mybir.dt.np(BF16)
    g = {k: np.asarray(v) for k, v in inputs.items()}
    experts = np.arange(F) // FE
    sel = (experts[None, :] == (np.arange(2 * E) % E)[:, None]).astype(np.float32)
    arrays = {
        "x": g["L0_attn_x"],
        "w_gate": g["L0_ffn_w_gate_proj"].reshape(F, D).T,
        "w_up": g["L0_ffn_w_up_proj"].reshape(F, D).T,
        "w_down": g["L0_ffn_w_down_proj"].transpose(0, 2, 1).reshape(F, D),
        "w_router": g["L0_ffn_w_gate_router"].T,
        "wq": g["L0_attn_WQ"], "wk": g["L0_attn_WK"], "wv": g["L0_attn_WV"], "proj": g["L0_attn_proj"],
        "bq": g["L0_attn_bQ"].reshape(R, NG, P).transpose(2, 0, 1),
        "bk": g["L0_attn_bK"].reshape(NG, P).T, "bv": g["L0_attn_bV"].reshape(NG, P).T,
        "ident_b": np.eye(P, dtype=np.float32).astype(bf16),
        "mask_b": np.triu(np.full((P, P), MASKED, np.float32), 1).astype(bf16),
        "sel": sel.reshape(2 * E, FB, P),
        "pair": np.tile(np.eye(E, dtype=np.float32), (2, 1)),
        "iota": np.tile(np.arange(E, dtype=np.float32), (P, CT)),
        "mhalf": np.full((P, CT), -0.5, np.float32),
        "eps": np.full((P, CT), EPS, np.float32),
        "ident": np.eye(P, dtype=np.float32),
    }
    nc = bacc.Bacc("TRN2", target_bir_lowering=False, num_devices=1)
    in_map, a = {}, {}
    for name, value in arrays.items():
        value = np.ascontiguousarray(value)
        in_map[f"in_{name}"] = value
        a[name] = nc.dram_tensor(f"in_{name}", value.shape, mybir.dt.from_np(value.dtype), kind="ExternalInput").ap()
    out = nc.dram_tensor("out", (B, T, D), F32, kind="ExternalOutput").ap()
    build(nc, a, out)
    r = run_bass_kernel_spmd(nc, [in_map], core_ids=[0])
    return r.results[0]["out"]
```

```python
from contextlib import ExitStack

import numpy as np

import concourse.bass as bass
from concourse import mybir

F32 = mybir.dt.float32
F32R = mybir.dt.float32r
BF16 = mybir.dt.bfloat16
U32 = mybir.dt.uint32
ALU = mybir.AluOpType
ACT = mybir.ActivationFunctionType
AX = mybir.AxisListType

P = 128
B, T, D = 4, 1024, 256
KD = D // P
TILES = B * T // P
E, FE = 8, 96
F = E * FE
FB = F // P
CT = 4
CN = CT * P
CHUNKS = TILES // CT
HS, NH, NG = 128, 16, 4
R = NH // NG
QT = T // P
EPS = 1e-5
MASKED = -3.0e38


def need(eng, sem, value):
    if isinstance(value, int) and value <= 0:
        return
    eng.wait_ge(sem, value)


class Chain:

    def __init__(self, nc, eng, sem, base, spare):
        self.nc, self.eng, self.sem, self.base, self.spare, self.n = nc, eng, sem, base, spare, 0

    def link(self, ins):
        self.n += 1
        ins.then_inc(self.sem, 1)

    def settle(self):
        self.eng.wait_ge(self.sem, self.base + self.n)

    def settle_first(self):
        self.settle()
        self.nc.vector.memset(self.spare, 0.0)


def split_terms(hi_a, lo_a, hi_b, lo_b):
    return [(hi_a, hi_b), (hi_a, lo_b), (lo_a, hi_b)]


def as_f32(ap):
    return ap.bitcast(F32)


def prep_buffers(sb):
    return {
        "stats": sb("stats", [P, CT, 6]), "mv": sb("mv", [P, CT, 2]), "veps": sb("veps", [P, CT]),
        "rstd": sb("rstd", [P, CT]), "xn": sb("xn", [P, CT, D]),
        "xt_hi": sb("xt_hi", [P, 2, KD, CN], F32R), "xt_lo": sb("xt_lo", [P, 2, KD, CN], F32R),
        "lg_t": sb("lg_t", [2 * E, CN]), "lg": sb("lg", [P, CT, E]),
        "top": sb("top", [P, CT, 8]), "top_i": sb("top_i", [P, CT, 8], U32), "top_f": sb("top_f", [P, CT, 2]),
        "gap": sb("gap", [P, CT]), "th": sb("th", [P, CT]), "spare": sb("spare", [P, 1]),
        "prob": sb("prob", [P, CT, 2]), "one1": sb("one1", [P, CT, E]), "one2": sb("one2", [P, CT, E]),
        "wtok": sb("wtok", [P, CT, E]), "wsp": sb("wsp", [P, CT, 2, E], F32R),
        "wt": sb("wt", [2 * E, 2, CN], F32R),
    }


class Prep:

    VSTEPS = 12
    TOP_VSTEPS = 8

    def __init__(self, nc, x, consts, w, buf, sem, x_in=None):
        self.nc, self.x, self.consts, self.w, self.x_in = nc, x, consts, w, x_in
        self.buf = buf
        self.stats_done, self.rstd_done, self.xn_done = sem("stats_done"), sem("rstd_done"), sem("xn_done")
        self.xt_made, self.xt_hi_done, self.xt_lo_done = sem("xt_made"), sem("xt_hi_done"), sem("xt_lo_done")
        self.lg_made, self.lg_t_done, self.lg_tok_made = sem("lg_made"), sem("lg_t_done"), sem("lg_tok_made")
        self.gap_done, self.th_done, self.wsp_done = sem("gap_done"), sem("th_done"), sem("wsp_done")
        self.wt_made, self.wt_done = sem("wt_made"), sem("wt_done")
        self.consts_set = sem("consts_set")
        self.statstep, self.vstep, self.pstep = sem("statstep"), sem("vstep"), sem("pstep")

    def rstd_of(self, pool, c):
        nc, buf = self.nc, self.buf
        pool.wait_ge(self.stats_done, c + 1)
        nc.gpsimd.tensor_tensor(buf["veps"][:, :], buf["mv"][:, :, 1], self.consts["eps"][:, :],
                                ALU.add).then_inc(self.pstep, 1)
        pool.wait_ge(self.pstep, c + 1)
        nc.gpsimd.tensor_tensor(buf["rstd"][:, :], buf["veps"][:, :], self.consts["mhalf"][:, :],
                                ALU.pow).then_inc(self.rstd_done, 1)

    def xt_high(self, act, c, par, k, bank):
        act.wait_ge(self.xt_made, KD * c + k + 1)
        self.nc.scalar.activation(self.buf["xt_hi"][:, par, k, :], bank, ACT.Copy).then_inc(self.xt_hi_done, 1)

    def logits_out(self, act, c, bank):
        act.wait_ge(self.lg_made, c + 1)
        self.nc.scalar.activation(self.buf["lg_t"][:, :], bank[0:2 * E, :], ACT.Copy).then_inc(self.lg_t_done, 1)

    def tanh(self, act, c):
        act.wait_ge(self.gap_done, c + 1)
        self.nc.scalar.activation(self.buf["th"][:, :], self.buf["gap"][:, :], ACT.Tanh, scale=0.5).then_inc(self.th_done, 1)

    def weights_out(self, act, c, par, bank):
        act.wait_ge(self.wt_made, c + 1)
        self.nc.scalar.activation(self.buf["wt"][:, par, :], bank[0:2 * E, :], ACT.Copy).then_inc(self.wt_done, 1)

    def statistics(self, dve, c):
        nc, buf = self.nc, self.buf
        if self.x_in is not None:
            dve.wait_ge(self.x_in, 16 * (c + 1))
        chain = Chain(nc, dve, self.statstep, CT * c, buf["spare"][:, :])
        for k in range(CT):
            chain.link(nc.vector.bn_stats(buf["stats"][:, k, :], self.x[:, c * CT + k, :]))
        chain.settle_first()
        for k in range(CT):
            last = nc.vector.bn_aggr(buf["mv"][:, k, :], buf["stats"][:, k, :])
        last.then_inc(self.stats_done, 1)

    def normalise(self, dve, c):
        buf = self.buf
        dve.wait_ge(self.rstd_done, c + 1)
        need(dve, self.xt_made, KD * c)
        for k in range(CT):
            last = self.nc.vector.tensor_scalar(buf["xn"][:, k, :], self.x[:, c * CT + k, :], buf["mv"][:, k, 0:1],
                                                buf["rstd"][:, k:k + 1], ALU.subtract, ALU.mult)
        last.then_inc(self.xn_done, 1)

    def xt_low(self, dve, c, par, k, bank):
        dve.wait_ge(self.xt_hi_done, KD * c + k + 1)
        self.nc.vector.tensor_tensor(self.buf["xt_lo"][:, par, k, :], bank, as_f32(self.buf["xt_hi"][:, par, k, :]),
                                     ALU.subtract).then_inc(self.xt_lo_done, 1)

    def top_two(self, dve, c, bank):
        nc, buf = self.nc, self.buf
        lg, top, top_i = buf["lg"], buf["top"], buf["top_i"]
        chain = Chain(nc, dve, self.vstep, self.VSTEPS * c, buf["spare"][:, :])
        dve.wait_ge(self.lg_tok_made, c + 1)
        chain.link(nc.vector.tensor_copy(lg[:, :, :], bank[:, 0:CT * E].rearrange("p (k e) -> p k e", e=E)))
        chain.settle_first()
        for k in range(CT):
            chain.link(nc.vector.max(top[:, k, :], lg[:, k, :]))
        chain.settle()
        nc.vector.tensor_tensor(buf["gap"][:, :], top[:, :, 0], top[:, :, 1], ALU.subtract).then_inc(self.gap_done, 1)
        for k in range(CT):
            last = nc.vector.max_index(top_i[:, k, :], top[:, k, :], lg[:, k, :])
        chain.link(last)
        chain.settle()
        chain.link(nc.vector.tensor_copy(buf["top_f"][:, :, :], top_i[:, :, 0:2]))
        chain.settle()
        i8 = self.consts["iota"][:, :].rearrange("p (k e) -> p k e", e=E)
        for r in range(2):
            last = nc.vector.tensor_tensor(buf[f"one{r + 1}"][:, :, :], i8,
                                           buf["top_f"][:, :, r:r + 1].broadcast_to([P, CT, E]), ALU.is_equal)
        chain.link(last)
        assert chain.n == self.TOP_VSTEPS

    def token_weights(self, dve, c):
        nc, buf = self.nc, self.buf
        prob, one1, one2, wtok, wsp = (buf[n] for n in ("prob", "one1", "one2", "wtok", "wsp"))
        chain = Chain(nc, dve, self.vstep, self.VSTEPS * c + self.TOP_VSTEPS, buf["spare"][:, :])
        dve.wait_ge(self.th_done, c + 1)
        nc.vector.tensor_scalar(prob[:, :, 0], buf["th"][:, :], 0.25, 0.25, ALU.mult, ALU.add)
        chain.link(nc.vector.tensor_scalar(prob[:, :, 1], buf["th"][:, :], -0.25, 0.25, ALU.mult, ALU.add))
        chain.settle()
        nc.vector.tensor_tensor(one1[:, :, :], one1[:, :, :], prob[:, :, 0:1].broadcast_to([P, CT, E]), ALU.mult)
        chain.link(nc.vector.tensor_tensor(one2[:, :, :], one2[:, :, :],
                                           prob[:, :, 1:2].broadcast_to([P, CT, E]), ALU.mult))
        chain.settle()
        chain.link(nc.vector.tensor_tensor(wtok[:, :, :], one1[:, :, :], one2[:, :, :], ALU.add))
        chain.settle()
        chain.link(nc.vector.tensor_copy(wsp[:, :, 0, :], wtok[:, :, :]))
        chain.settle()
        assert self.TOP_VSTEPS + chain.n == self.VSTEPS
        nc.vector.tensor_tensor(wsp[:, :, 1, :], wtok[:, :, :], as_f32(wsp[:, :, 0, :]),
                                ALU.subtract).then_inc(self.wsp_done, 1)

    def transposes(self, pe, c, k, bank):
        pe.wait_ge(self.xn_done, c + 1)
        if k > 0:
            pe.wait_ge(self.xt_lo_done, KD * c + k)
        self.transpose(c, k, bank)

    def transpose(self, c, k, bank):
        for t in range(CT):
            last = self.nc.tensor.transpose(bank[:, t * P:(t + 1) * P], self.buf["xn"][:, t, k * P:(k + 1) * P],
                                            self.consts["ident"][:, :])
        last.then_inc(self.xt_made, 1)

    def logits(self, pe, c, par, bank):
        pe.wait_ge(self.xt_lo_done, KD * (c + 1))
        terms = [(k, self.buf[xt]) for xt in ("xt_hi", "xt_lo") for k in range(KD)]
        for i, (k, xt) in enumerate(terms):
            last = self.nc.tensor.matmul(bank[0:2 * E, :], self.w["rt"][:, k, :], xt[:, par, k, :],
                                         start=i == 0, stop=i == len(terms) - 1)
        last.then_inc(self.lg_made, 1)

    def logits_by_token(self, pe, c, bank):
        pe.wait_ge(self.lg_t_done, c + 1)
        for t in range(CT):
            last = self.nc.tensor.matmul(bank[:, t * E:(t + 1) * E], self.buf["lg_t"][:, t * P:(t + 1) * P],
                                         self.consts["pair"][:, :], start=True, stop=True)
        last.then_inc(self.lg_tok_made, 1)

    def weights_by_feature(self, pe, c, bank):
        pe.wait_ge(self.wsp_done, c + 1)
        for t in range(CT):
            last = self.nc.tensor.transpose(bank[0:2 * E, t * P:(t + 1) * P],
                                            as_f32(self.buf["wsp"][:, t, :, :]).rearrange("p a e -> p (a e)"),
                                            self.consts["ident"][:, :])
        last.then_inc(self.wt_made, 1)


def moe_phase(nc, name, x, consts, w, banks, prep, load=None, store=None, fold=None, after=None):
    put_off = fold is None
    ident, sel, pair, iota = consts["ident"], consts["sel"], consts["pair"], consts["iota"]
    with ExitStack() as ctx:
        def sb(n, shape, dt=F32):
            return ctx.enter_context(nc.sbuf_tensor(f"{name}_{n}", shape, dt))

        def sem(n):
            return ctx.enter_context(nc.semaphore(f"{name}_{n}"))

        xt_hi, xt_lo, wt = prep.buf["xt_hi"], prep.buf["xt_lo"], prep.buf["wt"]
        sg = sb("sg", [P, 2, CN])
        gu = sb("gu", [P, 2, CN])
        hid = sb("hid", [P, 2, CN])
        h_hi = sb("h_hi", [P, 2, FB, CN], F32R)
        h_lo = sb("h_lo", [P, 2, FB, CN], F32R)

        gate_ps = [banks["s"][0][:, i * CN:(i + 1) * CN] for i in range(2)]
        up_ps = [banks["s"][1][:, i * CN:(i + 1) * CN] for i in range(2)]
        wb_ps, dn_ps, misc_ps = banks["q"][0][:, :], [banks["q"][1], banks["q"][2]], banks["q"][3][:, :]

        gate_made, up_made, wb_made = sem("gate_made"), sem("up_made"), sem("wb_made")
        silu_done, gu_done, hid_done = sem("silu_done"), sem("gu_done"), sem("hid_done")
        hi_done, lo_done = sem("hi_done"), sem("lo_done")
        dn_made, dn_free = sem("dn_made"), sem("dn_free")

        block = ctx.enter_context(nc.Block())

        if load is not None:
            raw_gu = sb("raw_gu", [P, KD, 2 * F])
            raw_dn = sb("raw_dn", [P, FB, D])
            raw_rt = sb("raw_rt", [P, KD, E])
            raw_sel = sb("raw_sel", [2 * E, FB, P], BF16)
            x_in = prep.x_in
            gate_in = [sem(f"gate_in{k}") for k in range(KD)]
            up_in = [sem(f"up_in{k}") for k in range(KD)]
            rt_in, dn_in, small_in, id_in = sem("rt_in"), sem("dn_in"), sem("small_in"), sem("id_in")
            whigh, wlow, sel_done = sem("whigh"), sem("wlow"), sem("sel_done")
            att_in, folded, rep_in = sem("att_in"), sem("folded"), [sem("wq_rep_in"), sem("proj_rep_in")]
            repeats = [raw_gu[:, :, :].rearrange("p k n -> p (k n)")[:, r * NG * D:(r + 1) * NG * D] for r in range(R - 1)]

            parts = [(rt_in, raw_rt[:, :, :], w["rt"][:, :, 0:E], w["rt"][:, :, E:2 * E])]
            for arrived, first_column in ((gate_in, 0), (up_in, F)):
                for k in range(KD):
                    cols = slice(first_column, first_column + F)
                    parts.append((arrived[k], raw_gu[:, k, cols], w["gu_hi"][:, k, cols], w["gu_lo"][:, k, cols]))
            parts.append((dn_in, raw_dn[:, :, :], w["dn_hi"][:, :, :], w["dn_lo"][:, :, :]))
            GATE_READY, UP_READY, DN_READY = 1 + KD, 1 + 2 * KD, 2 + 2 * KD

        if load is not None or store is not None:
            @block.sync
            def _(sp):
                if load is not None:
                    for c in range(CHUNKS):
                        sp.dma_start(x[:, c * CT:(c + 1) * CT, :], load["x"][:, c * CT:(c + 1) * CT, :]).then_inc(x_in, 16)
                        if c == 0:
                            sp.dma_start(ident[:, :], load["ident"]).then_inc(id_in, 16)
                        sp.wait_ge(x_in, 16 * (c + 1))
                    for n in ("ident_b", "mask_b"):
                        sp.dma_start(consts[n][:, :], load[n]).then_inc(att_in, 16)
                    for n in ("wq", "wk", "wv", "proj", "bq", "bk", "bv"):
                        sp.dma_start(load["attn"][n][0], load["attn"][n][1]).then_inc(att_in, 16)
                    sp.wait_ge(wlow, UP_READY)
                    for i, n in enumerate(("wq", "proj")):
                        if i:
                            sp.wait_ge(folded, R - 1)
                        for r in range(1, R):
                            sp.dma_start(repeats[r - 1], load["attn"][n + "_repeats"][r]).then_inc(rep_in[i], 16)
                if store is not None:
                    stores = [(c * CT, CT) for c in range(CHUNKS - 1)] + [(t, 1) for t in range(TILES - CT, TILES)]
                    for t, n in stores:
                        sp.wait_ge(dn_free, t + n + 2)
                        sp.dma_start(store["out"][:, t:t + n, :], x[:, t:t + n, :]).then_inc(store["sem"], 16)
                    sp.wait_ge(store["sem"], 16 * len(stores))

        @block.gpsimd
        def _(pool):
            if load is not None:
                nc.gpsimd.memset(consts["eps"][:, :], EPS).then_inc(prep.consts_set, 1)
                nc.gpsimd.memset(consts["mhalf"][:, :], -0.5).then_inc(prep.consts_set, 1)
                pool.wait_ge(prep.consts_set, 2)
                prep.rstd_of(pool, 0)
                prep.rstd_of(pool, 1)
            with pool.Fori(2, CHUNKS) as c:
                prep.rstd_of(pool, c)
            if load is not None:
                pool.wait_ge(att_in, 16 * 9)
                for i, total in enumerate((load["attn"]["wq"][0], load["attn"]["proj"][0])):
                    flat = total.rearrange("p g d -> p (g d)")
                    pool.wait_ge(rep_in[i], 16 * (R - 1))
                    for r in range(R - 1):
                        nc.gpsimd.tensor_tensor(flat, flat, repeats[r], ALU.add).then_inc(folded, 1)
                        pool.wait_ge(folded, i * (R - 1) + r + 1)
                bq = load["attn"]["bq"][0]
                for r in range(1, R):
                    nc.gpsimd.tensor_tensor(bq[:, 0, :], bq[:, 0, :], bq[:, r, :], ALU.add).then_inc(folded, 1)
                    pool.wait_ge(folded, 2 * (R - 1) + r)
                after.rstd_of(pool, 0)

        @block.scalar
        def _(act):
            if load is not None:
                act.dma_start(raw_rt[:, :, :], load["w_router"]).then_inc(rt_in, 16)
                for k in range(KD):
                    act.dma_start(raw_gu[:, k, 0:F], load["w_gate"][:, k, :]).then_inc(gate_in[k], 16)
                for k in range(KD):
                    act.dma_start(raw_gu[:, k, F:2 * F], load["w_up"][:, k, :]).then_inc(up_in[k], 16)
                act.dma_start(pair[:, :], load["pair"]).then_inc(small_in, 16)
                act.dma_start(iota[:, :], load["iota"]).then_inc(small_in, 16)
                act.dma_start(raw_sel[:, :, :], load["sel"]).then_inc(small_in, 16)
                act.dma_start(raw_dn[:, :, :], load["w_down"]).then_inc(dn_in, 16)

                def weight_high(n):
                    arrived, raw, high, _ = parts[n]
                    act.wait_ge(arrived, 16)
                    nc.scalar.activation(high, raw, ACT.Copy).then_inc(whigh, 1)

            def silu(c, fb):
                n = c * FB + fb
                act.wait_ge(gate_made, n + 1)
                need(act, gu_done, n - 1)
                nc.scalar.activation(sg[:, fb % 2, :], gate_ps[fb % 2], ACT.Silu).then_inc(silu_done, 1)

            def hi(c, par, fb):
                act.wait_ge(hid_done, c * FB + fb + 1)
                nc.scalar.activation(h_hi[:, par, fb, :], hid[:, fb % 2, :], ACT.Copy).then_inc(hi_done, 1)

            def chunk(c, par, last, first=False):
                if load is None or not first:
                    silu(c, 0)
                    if first:
                        prep.xt_high(act, c + 1, 1 - par, 0, misc_ps)
                    silu(c, 1)
                    hi(c, par, 0)
                    if first:
                        prep.xt_high(act, c + 1, 1 - par, 1, misc_ps)
                    hi(c, par, 1)
                if not last and not first:
                    prep.xt_high(act, c + 1, 1 - par, 0, misc_ps)
                    prep.xt_high(act, c + 1, 1 - par, 1, misc_ps)
                silu(c, 2)
                if not last:
                    prep.logits_out(act, c + 1, misc_ps)
                hi(c, par, 2)
                silu(c, 3)
                hi(c, par, 3)
                silu(c, 4)
                if not last:
                    prep.tanh(act, c + 1)
                hi(c, par, 4)
                silu(c, 5)
                if not last:
                    prep.weights_out(act, c + 1, 1 - par, misc_ps)
                hi(c, par, 5)

            if load is not None:
                for n in range(UP_READY):
                    weight_high(n)
                prep.xt_high(act, 0, 0, 0, misc_ps)
                prep.xt_high(act, 0, 0, 1, banks["q"][0][:, :])
                prep.logits_out(act, 0, misc_ps)
                silu(0, 0)
                act.wait_ge(small_in, 16 * 3)
                nc.scalar.activation(sel[:, :, :], raw_sel[:, :, :], ACT.Copy).then_inc(sel_done, 1)
                prep.tanh(act, 0)
                silu(0, 1)
                prep.weights_out(act, 0, 0, misc_ps)
                prep.xt_high(act, 1, 1, 0, misc_ps)
                hi(0, 0, 0)
                prep.xt_high(act, 1, 1, 1, misc_ps)
                hi(0, 0, 1)
                weight_high(UP_READY)
            chunk(0, 0, False, first=True)
            with act.Fori(0, (CHUNKS - 2) // 2) as j:
                chunk(2 * j + 1, 1, False)
                chunk(2 * j + 2, 0, False)
            chunk(CHUNKS - 1, 1, True)
            if fold is not None:
                fold.act(act)

        @block.vector
        def _(dve):
            if load is not None:
                def weight_low(n):
                    _, raw, high, low_part = parts[n]
                    dve.wait_ge(whigh, n + 1)
                    nc.vector.tensor_tensor(low_part, raw, as_f32(high), ALU.subtract).then_inc(wlow, 1)

            def gate_up(c, fb):
                n = c * FB + fb
                dve.wait_ge(silu_done, n + 1)
                dve.wait_ge(up_made, n + 1)
                nc.vector.tensor_tensor(gu[:, fb % 2, :], sg[:, fb % 2, :], up_ps[fb % 2], ALU.mult).then_inc(gu_done, 1)

            def weigh(c, fb):
                n = c * FB + fb
                dve.wait_ge(wb_made, n + 1)
                dve.wait_ge(gu_done, n + 1)
                nc.vector.tensor_tensor(hid[:, fb % 2, :], gu[:, fb % 2, :], wb_ps, ALU.mult).then_inc(hid_done, 1)

            def low(c, par, fb):
                n = c * FB + fb
                dve.wait_ge(hi_done, n + 1)
                nc.vector.tensor_tensor(h_lo[:, par, fb, :], hid[:, fb % 2, :], as_f32(h_hi[:, par, fb, :]),
                                        ALU.subtract).then_inc(lo_done, 1)

            def residual(c, k):
                dve.wait_ge(dn_made, CT * c + k + 1)
                nc.vector.tensor_tensor(x[:, c * CT + k, :], dn_ps[k % 2][:, 0:D], x[:, c * CT + k, :],
                                        ALU.add).then_inc(dn_free, 1)

            def chunk(c, par, first, last):
                opened = first and load is not None
                if not last and not first:
                    prep.statistics(dve, c + 1)
                if not opened:
                    gate_up(c, 0)
                if not first:
                    low(c - 1, 1 - par, FB - 1)
                weigh(c, 0)
                if first:
                    prep.xt_low(dve, c + 1, 1 - par, 0, misc_ps)
                elif not last:
                    prep.normalise(dve, c + 1)
                gate_up(c, 1)
                low(c, par, 0)
                weigh(c, 1)
                if first:
                    prep.xt_low(dve, c + 1, 1 - par, 1, misc_ps)
                low(c, par, 1)
                if opened:
                    weight_low(UP_READY)
                for k in range(CT):
                    if not first and not (put_off and last and k >= CT - KD):
                        residual(c - 1, k)
                    if not last and not first and k < KD:
                        prep.xt_low(dve, c + 1, 1 - par, k, misc_ps)
                gate_up(c, 2)
                weigh(c, 2)
                gate_up(c, 3)
                low(c, par, 2)
                weigh(c, 3)
                if not last:
                    prep.top_two(dve, c + 1, misc_ps)
                gate_up(c, 4)
                low(c, par, 3)
                weigh(c, 4)
                if not last:
                    prep.token_weights(dve, c + 1)
                gate_up(c, 5)
                low(c, par, 4)
                weigh(c, 5)

            nc.vector.memset(prep.buf["spare"][:, :], 0.0).then_inc(dn_free, 2)
            if load is not None:
                prep.statistics(dve, 0)
                for n in range(GATE_READY - 1):
                    weight_low(n)
                prep.normalise(dve, 0)
                weight_low(GATE_READY - 1)
                prep.xt_low(dve, 0, 0, 0, misc_ps)
                prep.xt_low(dve, 0, 0, 1, banks["q"][0][:, :])
                for n in range(GATE_READY, UP_READY):
                    weight_low(n)
                prep.statistics(dve, 1)
                dve.wait_ge(small_in, 16 * 3)
                prep.top_two(dve, 0, misc_ps)
                gate_up(0, 0)
                prep.token_weights(dve, 0)
                prep.normalise(dve, 1)
            chunk(0, 0, True, False)
            with dve.Fori(0, (CHUNKS - 2) // 2) as j:
                chunk(2 * j + 1, 1, False, False)
                chunk(2 * j + 2, 0, False, False)
            chunk(CHUNKS - 1, 1, False, True)
            low(CHUNKS - 1, 1, FB - 1)
            if fold is not None:
                after.statistics(dve, 0)
                after.normalise(dve, 0)
                fold.dve(dve)
            else:
                for k in range(CT - KD, CT):
                    residual(CHUNKS - 2, k)
            for k in range(CT):
                residual(CHUNKS - 1, k)

        @block.tensor
        def _(pe):
            def product(out, block_of, par):
                terms = [(k, a, b) for a, b in split_terms("gu_hi", "gu_lo", xt_hi, xt_lo) for k in range(KD)]
                for i, (k, a, b) in enumerate(terms):
                    last = nc.tensor.matmul(out, w[a][:, k, block_of], b[:, par, k, :],
                                            start=i == 0, stop=i == len(terms) - 1)
                return last

            def gate(c, par, fb):
                need(pe, silu_done, c * FB + fb - 1)
                product(gate_ps[fb % 2], slice(fb * P, (fb + 1) * P), par).then_inc(gate_made, 1)

            def up(c, par, fb):
                need(pe, gu_done, c * FB + fb - 1)
                product(up_ps[fb % 2], slice(F + fb * P, F + (fb + 1) * P), par).then_inc(up_made, 1)

            def weight(c, par, fb):
                need(pe, hid_done, c * FB + fb)
                if fb == 0:
                    pe.wait_ge(prep.wt_done, c + 1)
                nc.tensor.matmul(wb_ps, sel[:, fb, :], wt[:, par, :], start=True, stop=True).then_inc(wb_made, 1)

            def down(c, par, t):
                if t == 0:
                    pe.wait_ge(lo_done, FB * (c + 1))
                    if load is not None and isinstance(c, int) and c == 0:
                        pe.wait_ge(wlow, DN_READY)
                pe.wait_ge(dn_free, CT * c + t + 1)
                terms = [(fb, a, b) for fb in range(FB) for a, b in split_terms(h_hi, h_lo, "dn_hi", "dn_lo")]
                for i, (fb, a, b) in enumerate(terms):
                    last = nc.tensor.matmul(dn_ps[t % 2][:, 0:D], a[:, par, fb, t * P:(t + 1) * P], w[b][:, fb, :],
                                            start=i == 0, stop=i == len(terms) - 1)
                last.then_inc(dn_made, 1)

            def hidden(c, par, fb):
                gate(c, par, fb)
                up(c, par, fb)
                weight(c, par, fb)

            def chunk(c, par, first, last):
                if not (first and load is not None):
                    hidden(c, par, 0)
                if first:
                    prep.transposes(pe, c + 1, 0, misc_ps)
                if not (first and load is not None):
                    hidden(c, par, 1)
                else:
                    weight(c, par, 1)
                if first:
                    prep.transposes(pe, c + 1, 1, misc_ps)
                for t in range(CT):
                    if not first and not (put_off and last and t >= CT - KD):
                        down(c - 1, 1 - par, t)
                    if not last and not first and t < KD:
                        prep.transposes(pe, c + 1, t, misc_ps)
                hidden(c, par, 2)
                if not last:
                    prep.logits(pe, c + 1, 1 - par, misc_ps)
                hidden(c, par, 3)
                if not last:
                    prep.logits_by_token(pe, c + 1, misc_ps)
                hidden(c, par, 4)
                hidden(c, par, 5)
                if not last:
                    prep.weights_by_feature(pe, c + 1, misc_ps)

            if load is not None:
                pe.wait_ge(id_in, 16)
                prep.transposes(pe, 0, 0, misc_ps)
                prep.transposes(pe, 0, 1, banks["q"][0][:, :])
                pe.wait_ge(wlow, GATE_READY)
                prep.logits(pe, 0, 0, misc_ps)
                gate(0, 0, 0)
                pe.wait_ge(small_in, 16 * 3)
                prep.logits_by_token(pe, 0, misc_ps)
                pe.wait_ge(wlow, UP_READY)
                up(0, 0, 0)
                gate(0, 0, 1)
                up(0, 0, 1)
                prep.weights_by_feature(pe, 0, misc_ps)
                pe.wait_ge(sel_done, 1)
                weight(0, 0, 0)
            chunk(0, 0, True, False)
            with pe.Fori(0, (CHUNKS - 2) // 2) as j:
                chunk(2 * j + 1, 1, False, False)
                chunk(2 * j + 2, 0, False, False)
            chunk(CHUNKS - 1, 1, False, True)
            if fold is not None:
                pe.wait_ge(att_in, 16 * 9)
                pe.wait_ge(folded, 3 * (R - 1))
                fold.pe(pe, ((silu_done, CHUNKS * FB), (gu_done, CHUNKS * FB)))
                pe.wait_ge(hid_done, CHUNKS * FB)
                pe.wait_ge(after.xn_done, 1)
                for k, bank in enumerate(first_transposes_banks(banks)):
                    after.transpose(0, k, bank)
            if put_off:
                for t in range(CT - KD, CT):
                    down(CHUNKS - 2, 0, t)
            for t in range(CT):
                down(CHUNKS - 1, 1, t)


class Fold:

    VW = D + 2

    def __init__(self, nc, aw, banks, sb, sem):
        self.nc, self.aw, self.banks = nc, aw, banks
        VW = self.VW
        self.a_hi, self.a_lo = sb("a_hi", [P, KD, D], F32R), sb("a_lo", [P, KD, D], F32R)
        self.b_hi, self.b_lo = sb("b_hi", [P, KD, VW], F32R), sb("b_lo", [P, KD, VW], F32R)
        self.b_f = sb("b_f", [P, KD, VW])
        self.y_bias, self.v_bias = sb("y_bias", [P, KD]), sb("v_bias", [P, D + 1])
        self.made, self.high, self.pad = sem("fold_made"), sem("fold_high"), sem("fold_pad")

    def pe(self, pe, used):
        def group(out, pairs):
            for n, (a, b) in enumerate(pairs):
                last = self.nc.tensor.matmul(out, a, b, start=n == 0, stop=n == len(pairs) - 1)
            return last

        wq, wk, wv, proj, bq, bk, bv = (self.aw[n] for n in ("wq", "wk", "wv", "proj", "bq", "bk", "bv"))
        gs = range(NG)
        s0, s1, q3 = self.banks["s"][0], self.banks["s"][1], self.banks["q"][3]
        blocks = [slice(m * P, (m + 1) * P) for m in range(KD)]
        for m, d in enumerate(blocks):
            last = group(q3[:, m * D:(m + 1) * D], [(wq[:, g, d], wk[:, g, :]) for g in gs])
        last.then_inc(self.made, 1)
        for gates_and_ups_read in used:
            pe.wait_ge(*gates_and_ups_read)
        for m, d in enumerate(blocks):
            group(s0[:, m * CN:m * CN + D], [(wv[:, g, d], proj[:, g, :]) for g in gs])
            last = group(s0[:, m * CN + D:m * CN + D + 1], [(wq[:, g, d], bk[:, g:g + 1]) for g in gs])
        last.then_inc(self.made, 1)
        for m, d in enumerate(blocks):
            group(s1[:, D + 1 + m:D + 2 + m], [(wk[:, g, d], bq[:, 0, g:g + 1]) for g in gs])
        group(s1[:, 0:D], [(bv[:, g:g + 1].broadcast_to([P, P]), proj[:, g, :]) for g in gs])
        group(s1[:, D:D + 1], [(bq[:, 0, g:g + 1].broadcast_to([P, P]), bk[:, g:g + 1]) for g in gs]).then_inc(self.made, 1)

    def act(self, act):
        q3 = self.banks["q"][3][:, :].rearrange("p (m n) -> p m n", m=KD)
        s0 = self.banks["s"][0][:, :].rearrange("p (m n) -> p m n", m=KD)
        copy = self.nc.scalar.activation
        act.wait_ge(self.made, 1)
        copy(self.a_hi[:, :, :], q3, ACT.Copy).then_inc(self.high, 1)
        act.wait_ge(self.made, 2)
        copy(self.b_f[:, :, 0:D], s0[:, :, 0:D], ACT.Copy, scale=HS ** -0.5).then_inc(self.high, 1)
        copy(self.b_f[:, :, D:D + 1], s0[:, :, D:D + 1], ACT.Copy).then_inc(self.high, 1)
        act.wait_ge(self.high, 3)
        act.wait_ge(self.pad, 1)
        copy(self.b_hi[:, :, :], self.b_f[:, :, :], ACT.Copy).then_inc(self.high, 1)

    def dve(self, dve):
        q3 = self.banks["q"][3][:, :].rearrange("p (m n) -> p m n", m=KD)
        s1 = self.banks["s"][1]
        vector = self.nc.vector
        vector.memset(self.b_f[:, :, D + 1:], 0.0).then_inc(self.pad, 1)
        dve.wait_ge(self.high, 1)
        vector.tensor_tensor(self.a_lo[:, :, :], q3, as_f32(self.a_hi[:, :, :]), ALU.subtract)
        dve.wait_ge(self.made, 3)
        vector.tensor_copy(self.y_bias[:, :], s1[:, D + 1:D + 1 + KD])
        vector.tensor_scalar(self.v_bias[:, 0:D], s1[:, 0:D], HS ** -0.5, None, ALU.mult)
        vector.tensor_copy(self.v_bias[:, D:D + 1], s1[:, D:D + 1])
        dve.wait_ge(self.high, 4)
        vector.tensor_tensor(self.b_lo[:, :, :], self.b_f[:, :, :], as_f32(self.b_hi[:, :, :]), ALU.subtract)


def first_transposes_banks(banks):
    return [banks["q"][0][:, :], banks["s"][1][:, CN:]]


def attention_phase(nc, x, consts, fold, banks, first, prep):
    ident = consts["ident"]
    STEPS = B * QT
    AHEAD = CT
    VW = fold.VW
    RING = (QT + AHEAD) // CT
    VR = QT + 2
    a_hi, a_lo, b_hi, b_lo, y_bias, v_bias = fold.a_hi, fold.a_lo, fold.b_hi, fold.b_lo, fold.y_bias, fold.v_bias
    groups = [(i + CT) // CT for i in range(QT)]
    GROUPS = sum(groups)

    def group0(g):
        return g // QT * GROUPS + sum(groups[:g % QT])

    def place(t):
        return t // CT % RING, slice(t % CT * P, (t % CT + 1) * P)

    with ExitStack() as ctx:
        def sb(n, shape, dt=F32):
            return ctx.enter_context(nc.sbuf_tensor(f"att_{n}", shape, dt))

        def sem(n):
            return ctx.enter_context(nc.semaphore(f"att_{n}"))

        stats, mv = sb("stats", [P, 2, 6]), sb("mv", [P, 2, 2])
        veps, rstd = sb("veps", [P, 1]), sb("rstd", [P, 1])
        xn = sb("xn", [P, 2, D])
        xt_hi, xt_lo = sb("xt_hi", [P, RING, KD, CN], F32R), sb("xt_lo", [P, RING, KD, CN], F32R)
        yt_hi, yt_lo = sb("yt_hi", [P, 2, KD, 2 * P], F32R), sb("yt_lo", [P, 2, KD, 2 * P], F32R)
        v_f = sb("v_f", [P, 2, D])
        v_hi, v_lo = sb("v_hi", [P, VR, D], F32R), sb("v_lo", [P, VR, D], F32R)
        shift = sb("shift", [P, STEPS])
        neg_max, bias = sb("neg_max", [P, 2]), sb("bias", [P, 2])
        prob = sb("prob", [P, 2, T])
        total, inv = sb("total", [P, 2]), sb("inv", [P, 2])
        pt_hi, pt_lo = sb("pt_hi", [P, QT, P], F32R), sb("pt_lo", [P, QT, P], F32R)
        first.buf = {**first.buf, "xt_hi": xt_hi, "xt_lo": xt_lo}

        s_ps, pt_ps = banks["s"], banks["q"][0:2]
        pv_ps = banks["q"][2][:, 0:D]
        v_ps = banks["q"][3]

        def before_ps(g):
            return s_ps[(g + 1) % 2][:, CN:]

        def other_pt(g):
            return groups[(g - 1) % QT] == 1

        def t_ps(t):
            g = t - AHEAD
            bank = before_ps(g) if g % 2 == 0 else pt_ps[group0(g) % 2] if other_pt(g) else v_ps
            return bank[:, 0:D]

        def y_ps(p, m):
            return before_ps(2 * p - 1)[:, m * 2 * P:(m + 1) * 2 * P]

        first_banks = first_transposes_banks(banks)
        prep_bank = v_ps[:, :]
        prep_banks = [prep_bank, before_ps(STEPS - 2)]

        stats_made, stats_done, xn_done = sem("stats_made"), sem("stats_done"), sem("xn_done")
        pstep = sem("pstep")
        t_made, xt_hi_done, xt_lo_done = sem("t_made"), sem("xt_hi_done"), sem("xt_lo_done")
        y_made, y_hi_done, y_lo_done = sem("y_made"), sem("y_hi_done"), sem("y_lo_done")
        v_made, shift_done, v_f_done, v_hi_done, v_done = (sem(n) for n in ("v_made", "shift_done", "v_f_done", "v_hi_done", "v_done"))
        s_made, max_done, bias_done, exp_done = sem("s_made"), sem("max_done"), sem("bias_done"), sem("exp_done")
        pt_made, pt_hi_done, pt_lo_done = sem("pt_made"), sem("pt_hi_done"), sem("pt_lo_done")
        inv_done, pv_made, x_done = sem("inv_done"), sem("pv_made"), sem("x_done")

        block = ctx.enter_context(nc.Block())


        @block.gpsimd
        def _(pool):
            def normalise(t):
                n = t - CT
                pool.wait_ge(stats_done, n + 1)
                nc.gpsimd.tensor_tensor(veps[:, :], mv[:, n % 2, 1:2], consts["eps"][:, 0:1], ALU.add).then_inc(pstep, 1)
                pool.wait_ge(pstep, 2 * n + 1)
                nc.gpsimd.tensor_tensor(rstd[:, :], veps[:, :], consts["mhalf"][:, 0:1], ALU.pow).then_inc(pstep, 1)
                pool.wait_ge(pstep, 2 * n + 2)
                need(pool, t_made, n - 1)
                nc.gpsimd.tensor_scalar(xn[:, n % 2, :], x[:, t, :], mv[:, n % 2, 0:1], rstd[:, :],
                                        ALU.subtract, ALU.mult).then_inc(xn_done, 1)

            def v_low(t):
                pool.wait_ge(v_hi_done, t + 1)
                nc.gpsimd.tensor_tensor(v_lo[:, t % VR, :], v_f[:, t % 2, :], as_f32(v_hi[:, t % VR, :]),
                                        ALU.subtract).then_inc(v_done, 1)

            normalise(CT)
            v_low(0)
            for g in range(STEPS - 1):
                v_low(g + 1)
                if g + AHEAD + 1 < STEPS:
                    normalise(g + AHEAD + 1)
                if g == STEPS - CT:
                    prep.rstd_of(pool, 0)
            prep.rstd_of(pool, 1)

        @block.scalar
        def _(act):
            def xt_high(t):
                four, cols = place(t)
                act.wait_ge(t_made, t - CT + 1)
                nc.scalar.activation(xt_hi[:, four, :, cols], t_ps(t).rearrange("p (k c) -> p k c", k=KD),
                                     ACT.Copy).then_inc(xt_hi_done, 1)

            def y_high(p):
                act.wait_ge(y_made, p + 1)
                for m in range(KD):
                    last = nc.scalar.activation(yt_hi[:, p % 2, m, :], y_ps(p, m), ACT.Identity,
                                                bias=y_bias[:, m:m + 1])
                last.then_inc(y_hi_done, 1)

            def v_high(t):
                act.wait_ge(v_f_done, t + 1)
                nc.scalar.activation(v_hi[:, t % VR, :], v_f[:, t % 2, :], ACT.Copy).then_inc(v_hi_done, 1)

            def exps(g):
                n = (g % QT + 1) * P
                act.wait_ge(bias_done, g + 1)
                need(act, inv_done, g - 1)
                nc.scalar.activation(prob[:, g % 2, 0:n], s_ps[g % 2][:, 0:n], ACT.Exp, bias=bias[:, g % 2:g % 2 + 1],
                                     accum_out=total[:, g % 2:g % 2 + 1]).then_inc(exp_done, 1)

            def pt_high(g, r):
                k = min(CT, g % QT + 1 - r * CT)
                G = group0(g) + r
                act.wait_ge(pt_made, G + 1)
                nc.scalar.activation(pt_hi[:, r * CT:r * CT + k, :].rearrange("p k c -> p (k c)"),
                                     pt_ps[G % 2][:, 0:k * P], ACT.Copy).then_inc(pt_hi_done, 1)

            for k in range(KD):
                first.xt_high(act, 0, 0, k, first_banks[k])
            v_high(0)
            y_high(0)
            for g in range(STEPS + 1):
                if g == STEPS - 1:
                    prep.logits_out(act, 0, prep_bank)
                if g > 0:
                    for r in range(groups[(g - 1) % QT]):
                        pt_high(g - 1, r)
                if g + 1 < STEPS:
                    v_high(g + 1)
                if g == STEPS - 1:
                    prep.tanh(act, 0)
                if g + AHEAD < STEPS and g % 2 and other_pt(g):
                    xt_high(g + AHEAD)
                if g % 2 and g + 1 < STEPS:
                    y_high((g + 1) // 2)
                if g + AHEAD < STEPS and not (g % 2 and other_pt(g)):
                    xt_high(g + AHEAD)
                if g == STEPS - 2:
                    for k in range(KD):
                        prep.xt_high(act, 0, 0, k, prep_banks[k])
                if g < STEPS:
                    exps(g)
            prep.weights_out(act, 0, 0, prep_bank)

        @block.vector
        def _(dve):
            def statistics(t):
                n = t - CT
                need(dve, xn_done, n - 1)
                nc.vector.bn_stats(stats[:, n % 2, :], x[:, t, :]).then_inc(stats_made, 1)
                dve.wait_ge(stats_made, n + 1)
                nc.vector.bn_aggr(mv[:, n % 2, :], stats[:, n % 2, :]).then_inc(stats_done, 1)

            def xt_low(t):
                four, cols = place(t)
                dve.wait_ge(xt_hi_done, t - CT + 1)
                nc.vector.tensor_tensor(xt_lo[:, four, :, cols], t_ps(t).rearrange("p (k c) -> p k c", k=KD),
                                        as_f32(xt_hi[:, four, :, cols]), ALU.subtract).then_inc(xt_lo_done, 1)

            def y_low(p):
                dve.wait_ge(y_hi_done, p + 1)
                for m in range(KD):
                    last = nc.vector.scalar_tensor_tensor(yt_lo[:, p % 2, m, :], y_ps(p, m),
                                                          y_bias[:, m:m + 1], as_f32(yt_hi[:, p % 2, m, :]),
                                                          ALU.add, ALU.subtract)
                last.then_inc(y_lo_done, 1)

            def v_value(t):
                dve.wait_ge(v_made, t + 1)
                need(dve, v_done, t - 1)
                nc.vector.tensor_tensor(shift[:, t:t + 1], v_ps[:, D:D + 1], v_bias[:, D:D + 1],
                                        ALU.add).then_inc(shift_done, 1)
                nc.vector.tensor_tensor(v_f[:, t % 2, :], v_ps[:, 0:D], v_bias[:, 0:D], ALU.add).then_inc(v_f_done, 1)

            def maximum(g):
                i = g % QT
                dve.wait_ge(s_made, g + 1)
                nc.vector.tensor_reduce(neg_max[:, g % 2:g % 2 + 1], s_ps[g % 2][:, 0:(i + 1) * P], AX.X, ALU.max,
                                        negate=True).then_inc(max_done, 1)

            def exp_bias(g):
                dve.wait_ge(max_done, g + 1)
                dve.wait_ge(shift_done, g + 1)
                c = shift[:, g:g + 1]
                nc.vector.tensor_scalar(bias[:, g % 2:g % 2 + 1], neg_max[:, g % 2:g % 2 + 1], c, c,
                                        ALU.subtract, ALU.add).then_inc(bias_done, 1)

            def pt_low(g, r):
                k = min(CT, g % QT + 1 - r * CT)
                G = group0(g) + r
                dve.wait_ge(pt_hi_done, G + 1)
                blocks = slice(r * CT, r * CT + k)
                nc.vector.tensor_tensor(pt_lo[:, blocks, :].rearrange("p k c -> p (k c)"), pt_ps[G % 2][:, 0:k * P],
                                        as_f32(pt_hi[:, blocks, :]).rearrange("p k c -> p (k c)"),
                                        ALU.subtract).then_inc(pt_lo_done, 1)

            def inverse(g):
                dve.wait_ge(exp_done, g + 1)
                nc.vector.reciprocal(inv[:, g % 2:g % 2 + 1], total[:, g % 2:g % 2 + 1]).then_inc(inv_done, 1)

            def residual(g):
                dve.wait_ge(pv_made, g + 1)
                dve.wait_ge(inv_done, g + 1)
                nc.vector.scalar_tensor_tensor(x[:, g, :], pv_ps, inv[:, g % 2:g % 2 + 1], x[:, g, :],
                                               ALU.mult, ALU.add).then_inc(x_done, 1)

            for k in range(KD):
                first.xt_low(dve, 0, 0, k, first_banks[k])
            statistics(CT)
            v_value(0)
            y_low(0)
            for g in range(STEPS + 1):
                if g + 1 < STEPS:
                    v_value(g + 1)
                if g > 0:
                    for r in range(groups[(g - 1) % QT]):
                        pt_low(g - 1, r)
                if g + AHEAD + 1 < STEPS:
                    statistics(g + AHEAD + 1)
                if g == STEPS - CT:
                    prep.statistics(dve, 0)
                if g == STEPS - CT + 1:
                    prep.normalise(dve, 0)
                if g == STEPS - 2:
                    prep.statistics(dve, 1)
                if g == STEPS - 1:
                    prep.top_two(dve, 0, prep_bank)
                    prep.token_weights(dve, 0)
                short = g % QT < CT
                if g % 2 and other_pt(g) and g + AHEAD < STEPS:
                    xt_low(g + AHEAD)
                if short and g < STEPS:
                    maximum(g)
                    exp_bias(g)
                if g % 2 and g + 1 < STEPS:
                    y_low((g + 1) // 2)
                if not (g % 2 and other_pt(g)) and g + AHEAD < STEPS:
                    xt_low(g + AHEAD)
                if g == STEPS - 2:
                    for k in range(KD):
                        prep.xt_low(dve, 0, 0, k, prep_banks[k])
                if not short and g < STEPS:
                    maximum(g)
                    exp_bias(g)
                if g > 0:
                    inverse(g - 1)
                if g == STEPS:
                    prep.normalise(dve, 1)
                if g > 0:
                    residual(g - 1)

        @block.tensor
        def _(pe):
            def group(out, pairs):
                for n, (a, b) in enumerate(pairs):
                    last = nc.tensor.matmul(out, a, b, start=n == 0, stop=n == len(pairs) - 1)
                return last

            def transposes(t):
                n, g = t - CT, t - AHEAD
                if g % 2 and other_pt(g):
                    need(pe, pt_lo_done, group0(g) - 1)
                elif g % 2:
                    pe.wait_ge(v_f_done, g + 2)
                else:
                    need(pe, exp_done, g)
                pe.wait_ge(xn_done, n + 1)
                for k in range(KD):
                    last = nc.tensor.transpose(t_ps(t)[:, k * P:(k + 1) * P], xn[:, n % 2, k * P:(k + 1) * P], ident[:, :])
                last.then_inc(t_made, 1)

            def y(p):
                need(pe, exp_done, 2 * p - 1)
                need(pe, xt_lo_done, 2 * p + 2 - CT)
                four, _ = place(2 * p)
                cols = slice(2 * p % CT * P, (2 * p % CT + 2) * P)
                for m in range(KD):
                    pairs = [(a[:, k, m * P:(m + 1) * P], t[:, four, k, cols])
                             for a, t in split_terms(a_hi, a_lo, xt_hi, xt_lo) for k in range(KD)]
                    last = group(y_ps(p, m), pairs)
                last.then_inc(y_made, 1)

            def v(t):
                four, cols = place(t)
                need(pe, v_f_done, t)
                need(pe, xt_lo_done, min((t - 1) // 2 * 2, STEPS - CT))
                pairs = [(a[:, four, k, cols], w[:, k, :])
                         for a, w in split_terms(xt_hi, xt_lo, b_hi, b_lo) for k in range(KD)]
                group(v_ps[:, 0:VW], pairs).then_inc(v_made, 1)

            def scores(g):
                i = g % QT
                need(pe, exp_done, g - 1)
                pe.wait_ge(y_lo_done, g // 2 + 1)
                need(pe, xt_lo_done, min(g, STEPS - CT))
                n = (i + 1) * P
                here = slice(i % 2 * P, (i % 2 + 1) * P)
                for c0 in range(0, n, CN):
                    width = min(CN, max(n - c0, 2 * P))
                    four, _ = place(g - i + c0 // P)
                    pairs = [(a[:, g // 2 % 2, k, here], t[:, four, k, 0:width])
                             for a, t in split_terms(yt_hi, yt_lo, xt_hi, xt_lo) for k in range(KD)]
                    for m, (q, keys) in enumerate(pairs):
                        nc.tensor.matmul(s_ps[g % 2][:, c0:c0 + width], q, keys, start=m == 0, stop=False,
                                         skip_group_check=True)
                last = nc.tensor.matmul(s_ps[g % 2][:, n - P:n], consts["ident_b"][:, :], consts["mask_b"][:, :],
                                        start=False, stop=True, skip_group_check=True)
                last.then_inc(s_made, 1)

            def prob_transposes(g):
                i = g % QT
                pe.wait_ge(exp_done, g + 1)
                need(pe, xt_lo_done, min(g + 1, STEPS - CT))
                for r in range(groups[i]):
                    G = group0(g) + r
                    need(pe, pt_lo_done, G - 1)
                    for k in range(r * CT, min(i + 1, (r + 1) * CT)):
                        last = nc.tensor.transpose(pt_ps[G % 2][:, (k - r * CT) * P:(k - r * CT + 1) * P],
                                                   prob[:, g % 2, k * P:(k + 1) * P], ident[:, :])
                    last.then_inc(pt_made, 1)

            def values(g):
                i = g % QT
                need(pe, x_done, g)
                pe.wait_ge(v_done, g + 1)
                for k in range(i + 1):
                    if k % CT == 0:
                        pe.wait_ge(pt_lo_done, group0(g) + k // CT + 1)
                    slot = (g - i + k) % VR
                    for m, (p, w) in enumerate(split_terms(pt_hi, pt_lo, v_hi, v_lo)):
                        last = nc.tensor.matmul(pv_ps, p[:, k, :], w[:, slot, :], start=k + m == 0,
                                                stop=k == i and m == 2)
                last.then_inc(pv_made, 1)

            pe.wait_ge(first.xt_lo_done, KD)
            v(0)
            y(0)
            for g in range(STEPS):
                if g == STEPS - 1:
                    prep.logits(pe, 0, 0, prep_bank)
                if g + 1 < STEPS:
                    v(g + 1)
                if g > 0:
                    prob_transposes(g - 1)
                if g == STEPS - 1:
                    prep.logits_by_token(pe, 0, prep_bank)
                if g % 2 and other_pt(g) and g + AHEAD < STEPS:
                    transposes(g + AHEAD)
                if g % 2 and g + 1 < STEPS:
                    y((g + 1) // 2)
                if not (g % 2 and other_pt(g)) and g + AHEAD < STEPS:
                    transposes(g + AHEAD)
                if g == STEPS - 2:
                    pe.wait_ge(v_f_done, STEPS)
                    for k in range(KD):
                        prep.transpose(0, k, prep_banks[k])
                scores(g)
                if g > 0:
                    values(g - 1)
            prob_transposes(STEPS - 1)
            prep.weights_by_feature(pe, 0, prep_bank)
            values(STEPS - 1)


def build(nc, a, out):
    with ExitStack() as ctx:
        def sb(n, shape, dt=F32):
            return ctx.enter_context(nc.sbuf_tensor(n, shape, dt))
        x = sb("x", [P, TILES, D])
        consts = {
            "ident": sb("ident", [P, P]),
            "sel": sb("sel", [2 * E, FB, P], F32R),
            "pair": sb("pair", [2 * E, E]),
            "iota": sb("iota", [P, CT * E]),
            "mhalf": sb("mhalf", [P, CT]),
            "eps": sb("eps", [P, CT]),
            "ident_b": sb("ident_b", [P, P], BF16), "mask_b": sb("mask_b", [P, P], BF16),
        }
        w = {
            "gu_hi": sb("gu_hi", [P, KD, 2 * F], F32R), "gu_lo": sb("gu_lo", [P, KD, 2 * F], F32R),
            "dn_hi": sb("dn_hi", [P, FB, D], F32R), "dn_lo": sb("dn_lo", [P, FB, D], F32R),
            "rt": sb("rt", [P, KD, 2 * E], F32R),
        }
        aw = {
            "wq": sb("wq", [P, NG, D]), "wk": sb("wk", [P, NG, D]), "wv": sb("wv", [P, NG, D]),
            "proj": sb("proj", [P, NG, D]),
            "bq": sb("bq", [P, R, NG]), "bk": sb("bk", [P, NG]), "bv": sb("bv", [P, NG]),
        }
        repeats = {n: a[n].rearrange("(r g h) d -> r h g d", h=P, g=NG) for n in ("wq", "proj")}
        attn = {
            "wq": (aw["wq"][:, :, :], repeats["wq"][0]), "proj": (aw["proj"][:, :, :], repeats["proj"][0]),
            "wq_repeats": repeats["wq"], "proj_repeats": repeats["proj"],
            "wk": (aw["wk"][:, :, :], a["wk"].rearrange("(g h) d -> h g d", h=P)),
            "wv": (aw["wv"][:, :, :], a["wv"].rearrange("(g h) d -> h g d", h=P)),
            "bq": (aw["bq"][:, :, :], a["bq"]), "bk": (aw["bk"][:, :], a["bk"]), "bv": (aw["bv"][:, :], a["bv"]),
        }
        load = {
            "attn": attn,
            "x": a["x"].rearrange("b (n p) d -> p (b n) d", p=P),
            "w_gate": a["w_gate"].rearrange("(k p) f -> p k f", p=P),
            "w_up": a["w_up"].rearrange("(k p) f -> p k f", p=P),
            "w_down": a["w_down"].rearrange("(k p) f -> p k f", p=P),
            "w_router": a["w_router"].rearrange("(k p) e -> p k e", p=P),
            "sel": a["sel"], "pair": a["pair"], "iota": a["iota"], "ident": a["ident"],
            "ident_b": a["ident_b"], "mask_b": a["mask_b"],
        }
        banks = {
            "s": [ctx.enter_context(nc.psum_tensor(f"s{i}", [P, T], F32)) for i in range(2)],
            "q": [ctx.enter_context(nc.psum_tensor(f"q{i}", [P, CN], F32)) for i in range(4)],
        }

        def sem(n):
            return ctx.enter_context(nc.semaphore(n))

        buf = prep_buffers(sb)
        fold = Fold(nc, aw, banks, sb, sem)
        moe1_prep, first, moe2_prep = (Prep(nc, x, consts, w, buf, lambda s, n=n: sem(f"{n}_{s}"), x_in)
                                       for n, x_in in (("prep1", sem("x_in")), ("first", None), ("prep2", None)))
        moe_phase(nc, "moe1", x, consts, w, banks, moe1_prep, load=load, fold=fold, after=first)
        attention_phase(nc, x, consts, fold, banks, first, moe2_prep)
        out_t = out.rearrange("b (n p) d -> p (b n) d", p=P)
        moe_phase(nc, "moe2", x, consts, w, banks, moe2_prep, store={"out": out_t, "sem": sem("stored")})


def kernel(**inputs):
    import concourse.bacc as bacc
    from concourse.bass_utils import run_bass_kernel_spmd

    bf16 = mybir.dt.np(BF16)
    g = {k: np.asarray(v) for k, v in inputs.items()}
    experts = np.arange(F) // FE
    sel = (experts[None, :] == (np.arange(2 * E) % E)[:, None]).astype(np.float32)
    arrays = {
        "x": g["L0_attn_x"],
        "w_gate": g["L0_ffn_w_gate_proj"].reshape(F, D).T,
        "w_up": g["L0_ffn_w_up_proj"].reshape(F, D).T,
        "w_down": g["L0_ffn_w_down_proj"].transpose(0, 2, 1).reshape(F, D),
        "w_router": g["L0_ffn_w_gate_router"].T,
        "wq": g["L0_attn_WQ"], "wk": g["L0_attn_WK"], "wv": g["L0_attn_WV"], "proj": g["L0_attn_proj"],
        "bq": g["L0_attn_bQ"].reshape(R, NG, P).transpose(2, 0, 1),
        "bk": g["L0_attn_bK"].reshape(NG, P).T, "bv": g["L0_attn_bV"].reshape(NG, P).T,
        "ident_b": np.eye(P, dtype=np.float32).astype(bf16),
        "mask_b": np.triu(np.full((P, P), MASKED, np.float32), 1).astype(bf16),
        "sel": sel.reshape(2 * E, FB, P).astype(bf16),
        "pair": np.tile(np.eye(E, dtype=np.float32), (2, 1)),
        "iota": np.tile(np.arange(E, dtype=np.float32), (P, CT)),
        "ident": np.eye(P, dtype=np.float32),
    }
    nc = bacc.Bacc("TRN2", target_bir_lowering=False, num_devices=1)
    in_map, a = {}, {}
    for name, value in arrays.items():
        value = np.ascontiguousarray(value)
        in_map[f"in_{name}"] = value
        a[name] = nc.dram_tensor(f"in_{name}", value.shape, mybir.dt.from_np(value.dtype), kind="ExternalInput").ap()
    out = nc.dram_tensor("out", (B, T, D), F32, kind="ExternalOutput").ap()
    build(nc, a, out)
    r = run_bass_kernel_spmd(nc, [in_map], core_ids=[0])
    return r.results[0]["out"]
```

```python
from contextlib import ExitStack

import numpy as np

import concourse.bass as bass
from concourse import mybir

F32 = mybir.dt.float32
F32R = mybir.dt.float32r
BF16 = mybir.dt.bfloat16
U32 = mybir.dt.uint32
ALU = mybir.AluOpType
ACT = mybir.ActivationFunctionType
AX = mybir.AxisListType

P = 128
B, T, D = 4, 1024, 256
KD = D // P
TILES = B * T // P
E, FE = 8, 96
F = E * FE
FB = F // P
CT = 4
CN = CT * P
CHUNKS = TILES // CT
HS, NH, NG = 128, 16, 4
R = NH // NG
QT = T // P
EPS = 1e-5
MASKED = -3.0e38


def need(eng, sem, value):
    if isinstance(value, int) and value <= 0:
        return
    eng.wait_ge(sem, value)


class Chain:

    def __init__(self, nc, eng, sem, base, spare):
        self.nc, self.eng, self.sem, self.base, self.spare, self.n = nc, eng, sem, base, spare, 0

    def link(self, ins):
        self.n += 1
        ins.then_inc(self.sem, 1)

    def settle(self):
        self.eng.wait_ge(self.sem, self.base + self.n)

    def settle_first(self):
        self.settle()
        self.nc.vector.memset(self.spare, 0.0)


def load_table(nc, act, warm, function):
    act.wait_ge(warm["set"], 1)
    nc.scalar.activation(warm["out"], warm["in"], function)


def split_terms(hi_a, lo_a, hi_b, lo_b):
    return [(hi_a, hi_b), (hi_a, lo_b), (lo_a, hi_b)]


def as_f32(ap):
    return ap.bitcast(F32)


def prep_buffers(sb):
    return {
        "stats": sb("stats", [P, CT, 6]), "mv": sb("mv", [P, CT, 2]), "veps": sb("veps", [P, CT]),
        "rstd": sb("rstd", [P, CT]), "xn": sb("xn", [P, CT, D]),
        "xt_hi": sb("xt_hi", [P, 2, KD, CN], F32R), "xt_lo": sb("xt_lo", [P, 2, KD, CN], F32R),
        "lg_t": sb("lg_t", [2 * E, CN]), "lg": sb("lg", [P, CT, E]),
        "top": sb("top", [P, CT, 8]), "top_i": sb("top_i", [P, CT, 8], U32), "top_f": sb("top_f", [P, CT, 2]),
        "gap": sb("gap", [P, CT]), "th": sb("th", [P, CT]), "spare": sb("spare", [P, 1]),
        "prob": sb("prob", [P, CT, 2]), "one1": sb("one1", [P, CT, E]), "one2": sb("one2", [P, CT, E]),
        "wtok": sb("wtok", [P, CT, E]), "wsp": sb("wsp", [P, CT, 2, E], F32R),
        "wt": sb("wt", [2 * E, 2, CN], F32R),
    }


class Prep:

    VSTEPS = 7

    def __init__(self, nc, x, consts, w, buf, sem, x_in=None):
        self.nc, self.x, self.consts, self.w, self.x_in = nc, x, consts, w, x_in
        self.buf = buf
        self.stats_done, self.rstd_done, self.xn_done = sem("stats_done"), sem("rstd_done"), sem("xn_done")
        self.xt_made, self.xt_hi_done, self.xt_lo_done = sem("xt_made"), sem("xt_hi_done"), sem("xt_lo_done")
        self.lg_made, self.lg_t_done, self.lg_tok_made = sem("lg_made"), sem("lg_t_done"), sem("lg_tok_made")
        self.gap_done, self.th_done, self.prob_done = sem("gap_done"), sem("th_done"), sem("prob_done")
        self.one_done, self.wstep, self.wsp_done = sem("one_done"), sem("wstep"), sem("wsp_done")
        self.wt_made, self.wt_done = sem("wt_made"), sem("wt_done")
        self.consts_set = sem("consts_set")
        self.statstep, self.vstep, self.pstep = sem("statstep"), sem("vstep"), sem("pstep")

    def rstd_of(self, pool, c):
        nc, buf = self.nc, self.buf
        pool.wait_ge(self.stats_done, c + 1)
        nc.gpsimd.tensor_tensor(buf["veps"][:, :], buf["mv"][:, :, 1], self.consts["eps"][:, :],
                                ALU.add).then_inc(self.pstep, 1)
        pool.wait_ge(self.pstep, c + 1)
        nc.gpsimd.tensor_tensor(buf["rstd"][:, :], buf["veps"][:, :], self.consts["mhalf"][:, :],
                                ALU.pow).then_inc(self.rstd_done, 1)

    def token_weights(self, pool, c):
        tt, buf = self.nc.gpsimd.tensor_tensor, self.buf
        prob, one1, one2, wtok, wsp = (buf[n] for n in ("prob", "one1", "one2", "wtok", "wsp"))
        steps = 4
        pool.wait_ge(self.one_done, c + 1)
        pool.wait_ge(self.prob_done, c + 1)
        tt(one1[:, :, :], one1[:, :, :], prob[:, :, 0:1].broadcast_to([P, CT, E]), ALU.mult).then_inc(self.wstep, 1)
        tt(one2[:, :, :], one2[:, :, :], prob[:, :, 1:2].broadcast_to([P, CT, E]), ALU.mult).then_inc(self.wstep, 1)
        pool.wait_ge(self.wstep, steps * c + 2)
        tt(wtok[:, :, :], one1[:, :, :], one2[:, :, :], ALU.add).then_inc(self.wstep, 1)
        tt(wsp[:, :, 0, :], one1[:, :, :], one2[:, :, :], ALU.add).then_inc(self.wstep, 1)
        pool.wait_ge(self.wstep, steps * (c + 1))
        tt(wsp[:, :, 1, :], wtok[:, :, :], as_f32(wsp[:, :, 0, :]), ALU.subtract).then_inc(self.wsp_done, 1)

    def xt_high(self, act, c, par, k, bank):
        act.wait_ge(self.xt_made, KD * c + k + 1)
        self.nc.scalar.activation(self.buf["xt_hi"][:, par, k, :], bank, ACT.Copy).then_inc(self.xt_hi_done, 1)

    def logits_out(self, act, c, bank):
        act.wait_ge(self.lg_made, c + 1)
        self.nc.scalar.activation(self.buf["lg_t"][:, :], bank[0:2 * E, :], ACT.Copy).then_inc(self.lg_t_done, 1)

    def pair_weights(self, act, c):
        buf, copy = self.buf, self.nc.scalar.activation
        act.wait_ge(self.gap_done, c + 1)
        copy(buf["th"][:, :], buf["gap"][:, :], ACT.Tanh, scale=0.5).then_inc(self.th_done, 1)
        act.wait_ge(self.th_done, c + 1)
        copy(buf["prob"][:, :, 0], buf["th"][:, :], ACT.Copy, bias=0.25, scale=0.25)
        copy(buf["prob"][:, :, 1], buf["th"][:, :], ACT.Copy, bias=0.25, scale=-0.25).then_inc(self.prob_done, 1)

    def weights_out(self, act, c, par, bank):
        act.wait_ge(self.wt_made, c + 1)
        self.nc.scalar.activation(self.buf["wt"][:, par, :], bank[0:2 * E, :], ACT.Copy).then_inc(self.wt_done, 1)

    def statistics(self, dve, c):
        nc, buf = self.nc, self.buf
        if self.x_in is not None:
            dve.wait_ge(self.x_in, 16 * (c + 1))
        chain = Chain(nc, dve, self.statstep, CT * c, buf["spare"][:, :])
        for k in range(CT):
            chain.link(nc.vector.bn_stats(buf["stats"][:, k, :], self.x[:, c * CT + k, :]))
        chain.settle_first()
        for k in range(CT):
            last = nc.vector.bn_aggr(buf["mv"][:, k, :], buf["stats"][:, k, :])
        last.then_inc(self.stats_done, 1)

    def normalise(self, dve, c):
        buf = self.buf
        dve.wait_ge(self.rstd_done, c + 1)
        need(dve, self.xt_made, KD * c)
        for k in range(CT):
            last = self.nc.vector.tensor_scalar(buf["xn"][:, k, :], self.x[:, c * CT + k, :], buf["mv"][:, k, 0:1],
                                                buf["rstd"][:, k:k + 1], ALU.subtract, ALU.mult)
        last.then_inc(self.xn_done, 1)

    def xt_low(self, dve, c, par, k, bank):
        dve.wait_ge(self.xt_hi_done, KD * c + k + 1)
        self.nc.vector.tensor_tensor(self.buf["xt_lo"][:, par, k, :], bank, as_f32(self.buf["xt_hi"][:, par, k, :]),
                                     ALU.subtract).then_inc(self.xt_lo_done, 1)

    def top_two(self, dve, c, bank):
        nc, buf = self.nc, self.buf
        lg, top, top_i = buf["lg"], buf["top"], buf["top_i"]
        chain = Chain(nc, dve, self.vstep, self.VSTEPS * c, buf["spare"][:, :])
        dve.wait_ge(self.lg_tok_made, c + 1)
        parts = bank[:, 0:CT * 2 * E].rearrange("p (k a e) -> p k e a", a=2, e=E)
        chain.link(nc.vector.tensor_reduce(lg[:, :, :], parts, AX.X, ALU.add))
        chain.settle_first()
        for k in range(CT):
            chain.link(nc.vector.max(top[:, k, :], lg[:, k, :]))
        chain.settle()
        nc.vector.tensor_tensor(buf["gap"][:, :], top[:, :, 0], top[:, :, 1], ALU.subtract).then_inc(self.gap_done, 1)
        for k in range(CT):
            last = nc.vector.max_index(top_i[:, k, :], top[:, k, :], lg[:, k, :])
        chain.link(last)
        chain.settle()
        chain.link(nc.vector.tensor_copy(buf["top_f"][:, :, :], top_i[:, :, 0:2]))
        chain.settle()
        i8 = self.consts["iota"][:, :].rearrange("p (k e) -> p k e", e=E)
        for r in range(2):
            last = nc.vector.tensor_tensor(buf[f"one{r + 1}"][:, :, :], i8,
                                           buf["top_f"][:, :, r:r + 1].broadcast_to([P, CT, E]), ALU.is_equal)
        last.then_inc(self.one_done, 1)
        assert chain.n == self.VSTEPS

    def transposes(self, pe, c, k, bank):
        pe.wait_ge(self.xn_done, c + 1)
        if k > 0:
            pe.wait_ge(self.xt_lo_done, KD * c + k)
        self.transpose(c, k, bank)

    def transpose(self, c, k, bank):
        for t in range(CT):
            last = self.nc.tensor.transpose(bank[:, t * P:(t + 1) * P], self.buf["xn"][:, t, k * P:(k + 1) * P],
                                            self.consts["ident"][:, :])
        last.then_inc(self.xt_made, 1)

    def logits(self, pe, c, par, bank):
        pe.wait_ge(self.xt_lo_done, KD * (c + 1))
        terms = [(k, self.buf[xt]) for xt in ("xt_hi", "xt_lo") for k in range(KD)]
        for i, (k, xt) in enumerate(terms):
            last = self.nc.tensor.matmul(bank[0:2 * E, :], self.w["rt"][:, k, :], xt[:, par, k, :],
                                         start=i == 0, stop=i == len(terms) - 1)
        last.then_inc(self.lg_made, 1)

    def logits_by_token(self, pe, c, bank, waited=False):
        if not waited:
            pe.wait_ge(self.lg_t_done, c + 1)
        for t in range(CT):
            last = self.nc.tensor.transpose(bank[:, t * 2 * E:(t + 1) * 2 * E], self.buf["lg_t"][:, t * P:(t + 1) * P],
                                            self.consts["ident"][0:2 * E, 0:2 * E])
        last.then_inc(self.lg_tok_made, 1)

    def weights_by_feature(self, pe, c, bank):
        pe.wait_ge(self.wsp_done, c + 1)
        for t in range(CT):
            last = self.nc.tensor.transpose(bank[0:2 * E, t * P:(t + 1) * P],
                                            as_f32(self.buf["wsp"][:, t, :, :]).rearrange("p a e -> p (a e)"),
                                            self.consts["ident"][:, :])
        last.then_inc(self.wt_made, 1)


def moe_phase(nc, name, x, consts, w, banks, prep, warm, load=None, store=None, fold=None, after=None):
    put_off = fold is None
    ident, sel, iota = consts["ident"], consts["sel"], consts["iota"]
    with ExitStack() as ctx:
        def sb(n, shape, dt=F32):
            return ctx.enter_context(nc.sbuf_tensor(f"{name}_{n}", shape, dt))

        def sem(n):
            return ctx.enter_context(nc.semaphore(f"{name}_{n}"))

        xt_hi, xt_lo, wt = prep.buf["xt_hi"], prep.buf["xt_lo"], prep.buf["wt"]
        sg = sb("sg", [P, 2, CN])
        gu = sb("gu", [P, 2, CN])
        hid = sb("hid", [P, 2, CN])
        h_hi = sb("h_hi", [P, 2, FB, CN], F32R)
        h_lo = sb("h_lo", [P, 2, FB, CN], F32R)

        gate_ps = [banks["s"][0][:, i * CN:(i + 1) * CN] for i in range(2)]
        up_ps = [banks["s"][1][:, i * CN:(i + 1) * CN] for i in range(2)]
        wb_ps, dn_ps, misc_ps = banks["q"][0][:, :], [banks["q"][1], banks["q"][2]], banks["q"][3][:, :]

        gate_made, up_made, wb_made = sem("gate_made"), sem("up_made"), sem("wb_made")
        silu_done, gu_done, hid_done = sem("silu_done"), sem("gu_done"), sem("hid_done")
        hi_done, lo_done = sem("hi_done"), sem("lo_done")
        dn_made, dn_free = sem("dn_made"), sem("dn_free")

        block = ctx.enter_context(nc.Block())

        if load is not None:
            raw_gu = sb("raw_gu", [P, KD, 2 * F])
            raw_dn = sb("raw_dn", [P, FB, D])
            raw_rt = sb("raw_rt", [P, KD, E])
            raw_sel = sb("raw_sel", [2 * E, FB, P], BF16)
            x_in = prep.x_in
            gate_in = [sem(f"gate_in{k}") for k in range(KD)]
            up_in = [sem(f"up_in{k}") for k in range(KD)]
            rt_in, dn_in, small_in, id_in = sem("rt_in"), sem("dn_in"), sem("small_in"), sem("id_in")
            whigh, wlow, sel_done = sem("whigh"), sem("wlow"), sem("sel_done")
            att_in, folded, rep_in = sem("att_in"), sem("folded"), [sem("wq_rep_in"), sem("proj_rep_in")]
            repeats = [raw_gu[:, :, :].rearrange("p k n -> p (k n)")[:, r * NG * D:(r + 1) * NG * D] for r in range(R - 1)]

            parts = [(rt_in, raw_rt[:, :, :], w["rt"][:, :, 0:E], w["rt"][:, :, E:2 * E])]
            for arrived, first_column in ((gate_in, 0), (up_in, F)):
                for k in range(KD):
                    cols = slice(first_column, first_column + F)
                    parts.append((arrived[k], raw_gu[:, k, cols], w["gu_hi"][:, k, cols], w["gu_lo"][:, k, cols]))
            parts.append((dn_in, raw_dn[:, :, :], w["dn_hi"][:, :, :], w["dn_lo"][:, :, :]))
            GATE_READY, UP_READY, DN_READY = 1 + KD, 1 + 2 * KD, 2 + 2 * KD

        if load is not None or store is not None:
            @block.sync
            def _(sp):
                if load is not None:
                    for c in range(CHUNKS):
                        sp.dma_start(x[:, c * CT:(c + 1) * CT, :], load["x"][:, c * CT:(c + 1) * CT, :]).then_inc(x_in, 16)
                        if c == 0:
                            sp.dma_start(ident[:, :], load["ident"]).then_inc(id_in, 16)
                        sp.wait_ge(x_in, 16 * (c + 1))
                    for n in ("ident_b", "mask_b"):
                        sp.dma_start(consts[n][:, :], load[n]).then_inc(att_in, 16)
                    for n in ("wq", "wk", "wv", "proj", "bq", "bk", "bv"):
                        sp.dma_start(load["attn"][n][0], load["attn"][n][1]).then_inc(att_in, 16)
                    sp.wait_ge(wlow, UP_READY)
                    for i, n in enumerate(("wq", "proj")):
                        if i:
                            sp.wait_ge(folded, R - 1)
                        for r in range(1, R):
                            sp.dma_start(repeats[r - 1], load["attn"][n + "_repeats"][r]).then_inc(rep_in[i], 16)
                if store is not None:
                    stores = [(c * CT, CT) for c in range(CHUNKS - 1)] + [(t, 1) for t in range(TILES - CT, TILES)]
                    for t, n in stores:
                        sp.wait_ge(dn_free, t + n + 2)
                        sp.dma_start(store["out"][:, t:t + n, :], x[:, t:t + n, :]).then_inc(store["sem"], 16)
                    sp.wait_ge(store["sem"], 16 * len(stores))

        @block.gpsimd
        def _(pool):
            if load is not None:
                nc.gpsimd.memset(warm["in"], 0.0).then_inc(warm["set"], 1)
                nc.gpsimd.memset(consts["eps"][:, :], EPS).then_inc(prep.consts_set, 1)
                nc.gpsimd.memset(consts["mhalf"][:, :], -0.5).then_inc(prep.consts_set, 1)
                pool.wait_ge(prep.consts_set, 2)
                prep.rstd_of(pool, 0)
                prep.rstd_of(pool, 1)
                prep.token_weights(pool, 0)
            with pool.Fori(2, CHUNKS) as c:
                prep.rstd_of(pool, c)
                prep.token_weights(pool, c - 1)
            prep.token_weights(pool, CHUNKS - 1)
            if load is not None:
                pool.wait_ge(att_in, 16 * 9)
                for i, total in enumerate((load["attn"]["wq"][0], load["attn"]["proj"][0])):
                    flat = total.rearrange("p g d -> p (g d)")
                    pool.wait_ge(rep_in[i], 16 * (R - 1))
                    for r in range(R - 1):
                        nc.gpsimd.tensor_tensor(flat, flat, repeats[r], ALU.add).then_inc(folded, 1)
                        pool.wait_ge(folded, i * (R - 1) + r + 1)
                bq = load["attn"]["bq"][0]
                for r in range(1, R):
                    nc.gpsimd.tensor_tensor(bq[:, 0, :], bq[:, 0, :], bq[:, r, :], ALU.add).then_inc(folded, 1)
                    pool.wait_ge(folded, 2 * (R - 1) + r)
                nc.gpsimd.tensor_copy(fold.aw["wk"][:, :, D], load["attn"]["bk"][0]).then_inc(folded, 1)
                after.rstd_of(pool, 0)

        @block.scalar
        def _(act):
            if load is not None:
                act.dma_start(raw_rt[:, :, :], load["w_router"]).then_inc(rt_in, 16)
                for k in range(KD):
                    act.dma_start(raw_gu[:, k, 0:F], load["w_gate"][:, k, :]).then_inc(gate_in[k], 16)
                for k in range(KD):
                    act.dma_start(raw_gu[:, k, F:2 * F], load["w_up"][:, k, :]).then_inc(up_in[k], 16)
                act.dma_start(iota[:, :], load["iota"]).then_inc(small_in, 16)
                act.dma_start(raw_sel[:, :, :], load["sel"]).then_inc(small_in, 16)
                act.dma_start(raw_dn[:, :, :], load["w_down"]).then_inc(dn_in, 16)

                load_table(nc, act, warm, ACT.Silu)

                def weight_high(n):
                    arrived, raw, high, _ = parts[n]
                    act.wait_ge(arrived, 16)
                    nc.scalar.activation(high, raw, ACT.Copy).then_inc(whigh, 1)

            def silu(c, fb):
                n = c * FB + fb
                act.wait_ge(gate_made, n + 1)
                need(act, gu_done, n - 1)
                nc.scalar.activation(sg[:, fb % 2, :], gate_ps[fb % 2], ACT.Silu).then_inc(silu_done, 1)

            def hi(c, par, fb):
                act.wait_ge(hid_done, c * FB + fb + 1)
                nc.scalar.activation(h_hi[:, par, fb, :], hid[:, fb % 2, :], ACT.Copy).then_inc(hi_done, 1)

            def chunk(c, par, last, first=False):
                if load is None or not first:
                    silu(c, 0)
                    if first:
                        prep.xt_high(act, c + 1, 1 - par, 0, misc_ps)
                    silu(c, 1)
                    hi(c, par, 0)
                    if first:
                        prep.xt_high(act, c + 1, 1 - par, 1, misc_ps)
                    hi(c, par, 1)
                if not last and not first:
                    prep.xt_high(act, c + 1, 1 - par, 0, misc_ps)
                    prep.xt_high(act, c + 1, 1 - par, 1, misc_ps)
                silu(c, 2)
                if not last:
                    prep.logits_out(act, c + 1, misc_ps)
                hi(c, par, 2)
                silu(c, 3)
                hi(c, par, 3)
                silu(c, 4)
                if not last:
                    prep.pair_weights(act, c + 1)
                hi(c, par, 4)
                silu(c, 5)
                if not last:
                    prep.weights_out(act, c + 1, 1 - par, misc_ps)
                hi(c, par, 5)

            if load is not None:
                for n in range(GATE_READY):
                    weight_high(n)
                prep.xt_high(act, 0, 0, 0, misc_ps)
                prep.xt_high(act, 0, 0, 1, banks["q"][0][:, :])
                for n in range(GATE_READY, UP_READY):
                    weight_high(n)
                act.wait_ge(small_in, 16 * 2)
                nc.scalar.activation(sel[:, :, :], raw_sel[:, :, :], ACT.Copy).then_inc(sel_done, 1)
                prep.logits_out(act, 0, misc_ps)
                silu(0, 0)
                prep.pair_weights(act, 0)
                silu(0, 1)
                prep.weights_out(act, 0, 0, misc_ps)
                prep.xt_high(act, 1, 1, 0, misc_ps)
                hi(0, 0, 0)
                prep.xt_high(act, 1, 1, 1, misc_ps)
                hi(0, 0, 1)
                weight_high(UP_READY)
            chunk(0, 0, False, first=True)
            with act.Fori(0, (CHUNKS - 2) // 2) as j:
                chunk(2 * j + 1, 1, False)
                chunk(2 * j + 2, 0, False)
            chunk(CHUNKS - 1, 1, True)
            if fold is not None:
                fold.act(act)
                load_table(nc, act, warm, ACT.Exp)

        @block.vector
        def _(dve):
            if load is not None:
                def weight_low(n):
                    _, raw, high, low_part = parts[n]
                    dve.wait_ge(whigh, n + 1)
                    nc.vector.tensor_tensor(low_part, raw, as_f32(high), ALU.subtract).then_inc(wlow, 1)

            def gate_up(c, fb):
                n = c * FB + fb
                dve.wait_ge(silu_done, n + 1)
                dve.wait_ge(up_made, n + 1)
                nc.vector.tensor_tensor(gu[:, fb % 2, :], sg[:, fb % 2, :], up_ps[fb % 2], ALU.mult).then_inc(gu_done, 1)

            def weigh(c, fb):
                n = c * FB + fb
                dve.wait_ge(wb_made, n + 1)
                dve.wait_ge(gu_done, n + 1)
                nc.vector.tensor_tensor(hid[:, fb % 2, :], gu[:, fb % 2, :], wb_ps, ALU.mult).then_inc(hid_done, 1)

            def low(c, par, fb):
                n = c * FB + fb
                dve.wait_ge(hi_done, n + 1)
                nc.vector.tensor_tensor(h_lo[:, par, fb, :], hid[:, fb % 2, :], as_f32(h_hi[:, par, fb, :]),
                                        ALU.subtract).then_inc(lo_done, 1)

            def residual(c, k):
                dve.wait_ge(dn_made, CT * c + k + 1)
                nc.vector.tensor_tensor(x[:, c * CT + k, :], dn_ps[k % 2][:, 0:D], x[:, c * CT + k, :],
                                        ALU.add).then_inc(dn_free, 1)

            def chunk(c, par, first, last):
                opened = first and load is not None
                if not opened:
                    gate_up(c, 0)
                if not first:
                    low(c - 1, 1 - par, FB - 1)
                weigh(c, 0)
                if first:
                    prep.xt_low(dve, c + 1, 1 - par, 0, misc_ps)
                elif not last:
                    prep.normalise(dve, c + 1)
                gate_up(c, 1)
                low(c, par, 0)
                weigh(c, 1)
                if first:
                    prep.xt_low(dve, c + 1, 1 - par, 1, misc_ps)
                for k in range(CT):
                    if not first and not (put_off and last and k >= CT - KD):
                        residual(c - 1, k)
                    if k == 0:
                        low(c, par, 1)
                    if not last and not first and k % (CT // KD) == 0:
                        prep.xt_low(dve, c + 1, 1 - par, k // (CT // KD), misc_ps)
                if not (isinstance(c, int) and c + 2 >= CHUNKS):
                    prep.statistics(dve, c + 2)
                gate_up(c, 2)
                weigh(c, 2)
                gate_up(c, 3)
                low(c, par, 2)
                weigh(c, 3)
                if not last:
                    prep.top_two(dve, c + 1, misc_ps)
                gate_up(c, 4)
                low(c, par, 3)
                weigh(c, 4)
                if opened:
                    weight_low(UP_READY)
                gate_up(c, 5)
                low(c, par, 4)
                weigh(c, 5)

            nc.vector.memset(prep.buf["spare"][:, :], 0.0).then_inc(dn_free, 2)
            if load is not None:
                prep.statistics(dve, 0)
                prep.normalise(dve, 0)
                for n in range(GATE_READY):
                    weight_low(n)
                prep.xt_low(dve, 0, 0, 0, misc_ps)
                prep.xt_low(dve, 0, 0, 1, banks["q"][0][:, :])
                for n in range(GATE_READY, UP_READY):
                    weight_low(n)
                prep.statistics(dve, 1)
                dve.wait_ge(small_in, 16 * 2)
                prep.normalise(dve, 1)
                prep.top_two(dve, 0, misc_ps)
                gate_up(0, 0)
            chunk(0, 0, True, False)
            with dve.Fori(0, (CHUNKS - 4) // 2) as j:
                chunk(2 * j + 1, 1, False, False)
                chunk(2 * j + 2, 0, False, False)
            chunk(CHUNKS - 3, 1, False, False)
            chunk(CHUNKS - 2, 0, False, False)
            chunk(CHUNKS - 1, 1, False, True)
            low(CHUNKS - 1, 1, FB - 1)
            if fold is not None:
                after.statistics(dve, 0)
                after.normalise(dve, 0)
                fold.dve(dve)
            else:
                for k in range(CT - KD, CT):
                    residual(CHUNKS - 2, k)
            for k in range(CT):
                residual(CHUNKS - 1, k)

        @block.tensor
        def _(pe):
            def product(out, block_of, par):
                terms = [(k, a, b) for a, b in split_terms("gu_hi", "gu_lo", xt_hi, xt_lo) for k in range(KD)]
                for i, (k, a, b) in enumerate(terms):
                    last = nc.tensor.matmul(out, w[a][:, k, block_of], b[:, par, k, :],
                                            start=i == 0, stop=i == len(terms) - 1)
                return last

            def gate(c, par, fb):
                need(pe, silu_done, c * FB + fb - 1)
                product(gate_ps[fb % 2], slice(fb * P, (fb + 1) * P), par).then_inc(gate_made, 1)

            def up(c, par, fb):
                need(pe, gu_done, c * FB + fb - 1)
                product(up_ps[fb % 2], slice(F + fb * P, F + (fb + 1) * P), par).then_inc(up_made, 1)

            def weight(c, par, fb):
                need(pe, hid_done, c * FB + fb)
                if fb == 0:
                    pe.wait_ge(prep.wt_done, c + 1)
                nc.tensor.matmul(wb_ps, sel[:, fb, :], wt[:, par, :], start=True, stop=True).then_inc(wb_made, 1)

            def down(c, par, t):
                if t == 0:
                    pe.wait_ge(lo_done, FB * (c + 1))
                    if load is not None and isinstance(c, int) and c == 0:
                        pe.wait_ge(wlow, DN_READY)
                pe.wait_ge(dn_free, CT * c + t + 1)
                terms = [(fb, a, b) for fb in range(FB) for a, b in split_terms(h_hi, h_lo, "dn_hi", "dn_lo")]
                for i, (fb, a, b) in enumerate(terms):
                    last = nc.tensor.matmul(dn_ps[t % 2][:, 0:D], a[:, par, fb, t * P:(t + 1) * P], w[b][:, fb, :],
                                            start=i == 0, stop=i == len(terms) - 1)
                last.then_inc(dn_made, 1)

            def hidden(c, par, fb):
                gate(c, par, fb)
                up(c, par, fb)
                weight(c, par, fb)

            def chunk(c, par, first, last):
                if not (first and load is not None):
                    hidden(c, par, 0)
                if first:
                    prep.transposes(pe, c + 1, 0, misc_ps)
                if not (first and load is not None):
                    hidden(c, par, 1)
                else:
                    weight(c, par, 1)
                if first:
                    prep.transposes(pe, c + 1, 1, misc_ps)
                for t in range(CT):
                    if not first and not (put_off and last and t >= CT - KD):
                        down(c - 1, 1 - par, t)
                    if not last and not first and t % (CT // KD) == 0:
                        prep.transposes(pe, c + 1, t // (CT // KD), misc_ps)
                hidden(c, par, 2)
                if not last:
                    prep.logits(pe, c + 1, 1 - par, misc_ps)
                gate(c, par, 3)
                up(c, par, 3)
                if not last:
                    pe.wait_ge(prep.lg_t_done, c + 2)
                weight(c, par, 3)
                if not last:
                    prep.logits_by_token(pe, c + 1, misc_ps, waited=True)
                hidden(c, par, 4)
                hidden(c, par, 5)
                if not last:
                    prep.weights_by_feature(pe, c + 1, misc_ps)

            if load is not None:
                pe.wait_ge(id_in, 16)
                pe.wait_ge(prep.xn_done, 1)
                prep.transpose(0, 0, misc_ps)
                prep.transpose(0, 1, banks["q"][0][:, :])
                pe.wait_ge(wlow, GATE_READY)
                prep.logits(pe, 0, 0, misc_ps)
                gate(0, 0, 0)
                prep.logits_by_token(pe, 0, misc_ps)
                pe.wait_ge(wlow, UP_READY)
                up(0, 0, 0)
                gate(0, 0, 1)
                up(0, 0, 1)
                prep.weights_by_feature(pe, 0, misc_ps)
                pe.wait_ge(sel_done, 1)
                weight(0, 0, 0)
            chunk(0, 0, True, False)
            with pe.Fori(0, (CHUNKS - 2) // 2) as j:
                chunk(2 * j + 1, 1, False, False)
                chunk(2 * j + 2, 0, False, False)
            chunk(CHUNKS - 1, 1, False, True)
            if fold is not None:
                pe.wait_ge(att_in, 16 * 9)
                pe.wait_ge(folded, 3 * (R - 1) + 1)
                fold.pe(pe, [((silu_done, CHUNKS * FB - 1), (gu_done, CHUNKS * FB - 1)),
                             ((silu_done, CHUNKS * FB), (gu_done, CHUNKS * FB))])
                pe.wait_ge(hid_done, CHUNKS * FB)
                pe.wait_ge(after.xn_done, 1)
                for n, bank in enumerate(first_transposes_banks(banks)):
                    for k in range(KD):
                        for t in range(2):
                            last = nc.tensor.transpose(bank[:, (2 * k + t) * P:(2 * k + t + 1) * P],
                                                       after.buf["xn"][:, 2 * n + t, k * P:(k + 1) * P], ident[:, :])
                    last.then_inc(after.xt_made, 1)
            if put_off:
                for t in range(CT - KD, CT):
                    down(CHUNKS - 2, 0, t)
            for t in range(CT):
                down(CHUNKS - 1, 1, t)


class Fold:

    VW = D + 2

    def __init__(self, nc, aw, banks, sb, sem):
        self.nc, self.aw, self.banks = nc, aw, banks
        VW = self.VW
        self.a_hi, self.a_lo = sb("a_hi", [P, KD, D], F32R), sb("a_lo", [P, KD, D], F32R)
        self.b_hi, self.b_lo = sb("b_hi", [P, KD, VW], F32R), sb("b_lo", [P, KD, VW], F32R)
        self.b_f = sb("b_f", [P, KD, VW])
        self.y_bias, self.v_bias = sb("y_bias", [P, KD]), sb("v_bias", [P, D + 1])
        self.made, self.high, self.pad = sem("fold_made"), sem("fold_high"), sem("fold_pad")

    def pe(self, pe, used):
        def group(out, pairs):
            for n, (a, b) in enumerate(pairs):
                last = self.nc.tensor.matmul(out, a, b, start=n == 0, stop=n == len(pairs) - 1)
            return last

        wq, wk, wv, proj, bq, bv = (self.aw[n] for n in ("wq", "wk", "wv", "proj", "bq", "bv"))
        gs = range(NG)
        a_ps, b_ps, ybias_ps, cbias_ps, vbias_ps = self.places()
        blocks = [slice(m * P, (m + 1) * P) for m in range(KD)]
        for m, d in enumerate(blocks):
            group(ybias_ps[:, m:m + 1], [(wk[:, g, d], bq[:, 0, g:g + 1]) for g in gs])
        group(cbias_ps, [(bq[:, 0, g:g + 1].broadcast_to([P, P]), wk[:, g, D:D + 1]) for g in gs])
        for gates_and_ups_read in used[0]:
            pe.wait_ge(*gates_and_ups_read)
        for m, d in enumerate(blocks):
            last = group(a_ps[m], [(wq[:, g, d], wk[:, g, :]) for g in gs])
        last.then_inc(self.made, 1)
        group(vbias_ps, [(bv[:, g:g + 1].broadcast_to([P, P]), proj[:, g, :]) for g in gs])
        for gates_and_ups_read in used[1]:
            pe.wait_ge(*gates_and_ups_read)
        for m, d in enumerate(blocks):
            last = group(b_ps[m], [(wv[:, g, d], proj[:, g, :]) for g in gs])
        last.then_inc(self.made, 1)

    def places(self):
        s0, s1, q3 = self.banks["s"][0], self.banks["s"][1], self.banks["q"][3]
        return ([q3[:, 0:D + 1], s0[:, 0:D + 1]], [s1[:, 0:D], s0[:, CN:CN + D]],
                q3[:, D + 1:D + 1 + KD], q3[:, D + 1 + KD:D + 2 + KD], s1[:, D:2 * D])

    def act(self, act):
        a_ps, b_ps, *_ = self.places()
        copy = self.nc.scalar.activation
        act.wait_ge(self.made, 1)
        for m in range(KD):
            copy(self.a_hi[:, m, :], a_ps[m][:, 0:D], ACT.Copy)
            last = copy(self.b_f[:, m, D:D + 1], a_ps[m][:, D:D + 1], ACT.Copy)
        last.then_inc(self.high, 1)
        act.wait_ge(self.made, 2)
        for m in range(KD):
            last = copy(self.b_f[:, m, 0:D], b_ps[m], ACT.Copy, scale=HS ** -0.5)
        last.then_inc(self.high, 1)
        act.wait_ge(self.high, 2)
        act.wait_ge(self.pad, 1)
        copy(self.b_hi[:, :, :], self.b_f[:, :, :], ACT.Copy).then_inc(self.high, 1)

    def dve(self, dve):
        a_ps, _, ybias_ps, cbias_ps, vbias_ps = self.places()
        vector = self.nc.vector
        vector.memset(self.b_f[:, :, D + 1:], 0.0).then_inc(self.pad, 1)
        dve.wait_ge(self.high, 1)
        for m in range(KD):
            vector.tensor_tensor(self.a_lo[:, m, :], a_ps[m][:, 0:D], as_f32(self.a_hi[:, m, :]), ALU.subtract)
        vector.tensor_copy(self.y_bias[:, :], ybias_ps)
        vector.tensor_copy(self.v_bias[:, D:D + 1], cbias_ps)
        dve.wait_ge(self.high, 2)
        vector.tensor_scalar(self.v_bias[:, 0:D], vbias_ps, HS ** -0.5, None, ALU.mult)
        dve.wait_ge(self.high, 3)
        vector.tensor_tensor(self.b_lo[:, :, :], self.b_f[:, :, :], as_f32(self.b_hi[:, :, :]), ALU.subtract)


def first_transposes_banks(banks):
    return [banks["q"][0][:, :], banks["s"][1][:, CN:]]


def attention_phase(nc, x, consts, fold, banks, warm, first, prep):
    ident = consts["ident"]
    STEPS = B * QT
    AHEAD = CT
    VW = fold.VW
    RING = (QT + AHEAD) // CT
    VR = QT + 2
    a_hi, a_lo, b_hi, b_lo, y_bias, v_bias = fold.a_hi, fold.a_lo, fold.b_hi, fold.b_lo, fold.y_bias, fold.v_bias
    groups = [(i + CT) // CT for i in range(QT)]
    GROUPS = sum(groups)

    def group0(g):
        return g // QT * GROUPS + sum(groups[:g % QT])

    def place(t):
        return t // CT % RING, slice(t % CT * P, (t % CT + 1) * P)

    with ExitStack() as ctx:
        def sb(n, shape, dt=F32):
            return ctx.enter_context(nc.sbuf_tensor(f"att_{n}", shape, dt))

        def sem(n):
            return ctx.enter_context(nc.semaphore(f"att_{n}"))

        stats, mv = sb("stats", [P, 2, 6]), sb("mv", [P, 2, 2])
        veps, rstd = sb("veps", [P, 2]), sb("rstd", [P, 2])
        xn = sb("xn", [P, 2, D])
        xt_hi, xt_lo = sb("xt_hi", [P, RING, KD, CN], F32R), sb("xt_lo", [P, RING, KD, CN], F32R)
        yt_hi, yt_lo = sb("yt_hi", [P, 2, KD, 2 * P], F32R), sb("yt_lo", [P, 2, KD, 2 * P], F32R)
        v_f = sb("v_f", [P, 2, D])
        v_hi, v_lo = sb("v_hi", [P, VR, D], F32R), sb("v_lo", [P, VR, D], F32R)
        shift = sb("shift", [P, STEPS])
        neg_max, bias = sb("neg_max", [P, 2]), sb("bias", [P, 2])
        prob = sb("prob", [P, 2, T])
        total, inv = sb("total", [P, 2]), sb("inv", [P, 2])
        pt_hi, pt_lo = sb("pt_hi", [P, QT, P], F32R), sb("pt_lo", [P, QT, P], F32R)

        s_ps, pt_ps = banks["s"], banks["q"][0:2]
        pv_ps = banks["q"][2][:, 0:D]
        v_ps = banks["q"][3]

        def before_ps(g):
            return s_ps[(g + 1) % 2][:, CN:]

        def other_pt(g):
            return groups[(g - 1) % QT] == 1

        def t_ps(t):
            g = t - AHEAD
            bank = before_ps(g) if g % 2 == 0 else pt_ps[group0(g) % 2] if other_pt(g) else v_ps
            return bank[:, 0:D]

        def y_ps(p, m):
            return before_ps(2 * p - 1)[:, m * 2 * P:(m + 1) * 2 * P]

        firsts = [(slice(n * 2 * P, (n + 1) * 2 * P), bank.rearrange("p (k c) -> p k c", k=KD))
                  for n, bank in enumerate(first_transposes_banks(banks))]
        prep_bank = v_ps[:, :]
        prep_banks = [prep_bank, before_ps(STEPS - 2)]

        stats_made, stats_done, rstd_done, xn_done = (sem(n) for n in ("stats_made", "stats_done", "rstd_done", "xn_done"))
        pstep = sem("pstep")
        t_made, xt_hi_done, xt_lo_done = sem("t_made"), sem("xt_hi_done"), sem("xt_lo_done")
        y_made, y_hi_done, y_lo_done = sem("y_made"), sem("y_hi_done"), sem("y_lo_done")
        v_made, shift_done, v_f_done = sem("v_made"), sem("shift_done"), sem("v_f_done")
        v_hi_done, v_done = sem("v_hi_done"), sem("v_done")
        s_made, max_done, bias_done, exp_done = sem("s_made"), sem("max_done"), sem("bias_done"), sem("exp_done")
        pt_made, pt_hi_done, pt_lo_done = sem("pt_made"), sem("pt_hi_done"), sem("pt_lo_done")
        inv_done, pv_made, x_done = sem("inv_done"), sem("pv_made"), sem("x_done")

        def early(g):
            return 0 < g % QT <= CT

        block = ctx.enter_context(nc.Block())


        @block.gpsimd
        def _(pool):
            def rstd_of(t):
                n = t - CT
                pool.wait_ge(stats_done, n + 1)
                nc.gpsimd.tensor_tensor(veps[:, n % 2:n % 2 + 1], mv[:, n % 2, 1:2], consts["eps"][:, 0:1],
                                        ALU.add).then_inc(pstep, 1)
                pool.wait_ge(pstep, n + 1)
                need(pool, xn_done, n - 1)
                nc.gpsimd.tensor_tensor(rstd[:, n % 2:n % 2 + 1], veps[:, n % 2:n % 2 + 1], consts["mhalf"][:, 0:1],
                                        ALU.pow).then_inc(rstd_done, 1)

            def v_low(t):
                pool.wait_ge(v_hi_done, t + 1)
                nc.gpsimd.tensor_tensor(v_lo[:, t % VR, :], v_f[:, t % 2, :], as_f32(v_hi[:, t % VR, :]),
                                        ALU.subtract).then_inc(v_done, 1)

            rstd_of(CT)
            v_low(0)
            rstd_of(CT + 1)
            for g in range(STEPS - 1):
                v_low(g + 1)
                if g + AHEAD + 2 < STEPS:
                    rstd_of(g + AHEAD + 2)
                if g == STEPS - CT:
                    prep.rstd_of(pool, 0)
            prep.rstd_of(pool, 1)
            prep.token_weights(pool, 0)

        @block.scalar
        def _(act):
            def xt_high(t):
                four, cols = place(t)
                act.wait_ge(t_made, t - CT + 1)
                nc.scalar.activation(xt_hi[:, four, :, cols], t_ps(t).rearrange("p (k c) -> p k c", k=KD),
                                     ACT.Copy).then_inc(xt_hi_done, 1)

            def y_high(p):
                act.wait_ge(y_made, p + 1)
                for m in range(KD):
                    last = nc.scalar.activation(yt_hi[:, p % 2, m, :], y_ps(p, m), ACT.Identity,
                                                bias=y_bias[:, m:m + 1])
                last.then_inc(y_hi_done, 1)

            def v_high(t):
                act.wait_ge(v_f_done, t + 1)
                nc.scalar.activation(v_hi[:, t % VR, :], v_f[:, t % 2, :], ACT.Copy).then_inc(v_hi_done, 1)

            def exps(g):
                n = (g % QT + 1) * P
                act.wait_ge(bias_done, g + 1)
                need(act, inv_done, g - 1)
                nc.scalar.activation(prob[:, g % 2, 0:n], s_ps[g % 2][:, 0:n], ACT.Exp, bias=bias[:, g % 2:g % 2 + 1],
                                     accum_out=total[:, g % 2:g % 2 + 1]).then_inc(exp_done, 1)

            def pt_high(g, r):
                k = min(CT, g % QT + 1 - r * CT)
                G = group0(g) + r
                act.wait_ge(pt_made, G + 1)
                nc.scalar.activation(pt_hi[:, r * CT:r * CT + k, :].rearrange("p k c -> p (k c)"),
                                     pt_ps[G % 2][:, 0:k * P], ACT.Copy).then_inc(pt_hi_done, 1)

            for n, (half, bank) in enumerate(firsts):
                act.wait_ge(first.xt_made, n + 1)
                nc.scalar.activation(xt_hi[:, 0, :, half], bank, ACT.Copy).then_inc(first.xt_hi_done, 1)
            v_high(0)
            y_high(0)

            for g in range(STEPS + 1):
                if g == STEPS - 1:
                    prep.logits_out(act, 0, prep_bank)
                if early(g) and g + AHEAD < STEPS:
                    xt_high(g + AHEAD)
                if g > 0:
                    for r in range(groups[(g - 1) % QT]):
                        pt_high(g - 1, r)
                if not early(g):
                    if g + 1 < STEPS:
                        v_high(g + 1)
                    if g == STEPS - 1:
                        prep.pair_weights(act, 0)
                if g % 2 and g + 1 < STEPS:
                    y_high((g + 1) // 2)
                if early(g):
                    v_high(g + 1)
                elif g + AHEAD < STEPS:
                    xt_high(g + AHEAD)
                if g == STEPS - 2:
                    for k in range(KD):
                        prep.xt_high(act, 0, 0, k, prep_banks[k])
                if g < STEPS:
                    exps(g)
            prep.weights_out(act, 0, 0, prep_bank)
            load_table(nc, act, warm, ACT.Silu)

        @block.vector
        def _(dve):
            def statistics(t):
                n = t - CT
                need(dve, rstd_done, n - 1)
                nc.vector.bn_stats(stats[:, n % 2, :], x[:, t, :]).then_inc(stats_made, 1)
                dve.wait_ge(stats_made, n + 1)
                nc.vector.bn_aggr(mv[:, n % 2, :], stats[:, n % 2, :]).then_inc(stats_done, 1)

            def normalise(t):
                n = t - CT
                dve.wait_ge(rstd_done, n + 1)
                need(dve, t_made, n - 1)
                nc.vector.tensor_scalar(xn[:, n % 2, :], x[:, t, :], mv[:, n % 2, 0:1], rstd[:, n % 2:n % 2 + 1],
                                        ALU.subtract, ALU.mult).then_inc(xn_done, 1)

            def xt_low(t):
                four, cols = place(t)
                dve.wait_ge(xt_hi_done, t - CT + 1)
                nc.vector.tensor_tensor(xt_lo[:, four, :, cols], t_ps(t).rearrange("p (k c) -> p k c", k=KD),
                                        as_f32(xt_hi[:, four, :, cols]), ALU.subtract).then_inc(xt_lo_done, 1)

            def y_low(p):
                dve.wait_ge(y_hi_done, p + 1)
                for m in range(KD):
                    last = nc.vector.scalar_tensor_tensor(yt_lo[:, p % 2, m, :], y_ps(p, m),
                                                          y_bias[:, m:m + 1], as_f32(yt_hi[:, p % 2, m, :]),
                                                          ALU.add, ALU.subtract)
                last.then_inc(y_lo_done, 1)

            def v_value(t):
                dve.wait_ge(v_made, t + 1)
                need(dve, v_done, t - 1)
                nc.vector.tensor_tensor(shift[:, t:t + 1], v_ps[:, D:D + 1], v_bias[:, D:D + 1],
                                        ALU.add).then_inc(shift_done, 1)
                nc.vector.tensor_tensor(v_f[:, t % 2, :], v_ps[:, 0:D], v_bias[:, 0:D], ALU.add).then_inc(v_f_done, 1)

            def maximum(g):
                i = g % QT
                dve.wait_ge(s_made, g + 1)
                nc.vector.tensor_reduce(neg_max[:, g % 2:g % 2 + 1], s_ps[g % 2][:, 0:(i + 1) * P], AX.X, ALU.max,
                                        negate=True).then_inc(max_done, 1)

            def exp_bias(g):
                dve.wait_ge(max_done, g + 1)
                dve.wait_ge(shift_done, g + 1)
                c = shift[:, g:g + 1]
                nc.vector.tensor_scalar(bias[:, g % 2:g % 2 + 1], neg_max[:, g % 2:g % 2 + 1], c, c,
                                        ALU.subtract, ALU.add).then_inc(bias_done, 1)

            def pt_low(g, r):
                k = min(CT, g % QT + 1 - r * CT)
                G = group0(g) + r
                dve.wait_ge(pt_hi_done, G + 1)
                blocks = slice(r * CT, r * CT + k)
                nc.vector.tensor_tensor(pt_lo[:, blocks, :].rearrange("p k c -> p (k c)"), pt_ps[G % 2][:, 0:k * P],
                                        as_f32(pt_hi[:, blocks, :]).rearrange("p k c -> p (k c)"),
                                        ALU.subtract).then_inc(pt_lo_done, 1)

            def inverse(g):
                dve.wait_ge(exp_done, g + 1)
                nc.vector.reciprocal(inv[:, g % 2:g % 2 + 1], total[:, g % 2:g % 2 + 1]).then_inc(inv_done, 1)

            def residual(g):
                dve.wait_ge(pv_made, g + 1)
                dve.wait_ge(inv_done, g + 1)
                nc.vector.scalar_tensor_tensor(x[:, g, :], pv_ps, inv[:, g % 2:g % 2 + 1], x[:, g, :],
                                               ALU.mult, ALU.add).then_inc(x_done, 1)

            statistics(CT)
            for n, (half, bank) in enumerate(firsts):
                dve.wait_ge(first.xt_hi_done, n + 1)
                nc.vector.tensor_tensor(xt_lo[:, 0, :, half], bank, as_f32(xt_hi[:, 0, :, half]),
                                        ALU.subtract).then_inc(first.xt_lo_done, 1)
            normalise(CT)
            statistics(CT + 1)
            v_value(0)
            y_low(0)

            for g in range(STEPS + 1):
                if g + 1 < STEPS and not early(g):
                    v_value(g + 1)
                if early(g):
                    if g + AHEAD < STEPS:
                        xt_low(g + AHEAD)
                    if g > 1:
                        residual(g - 2)
                if g > 0:
                    for r in range(groups[(g - 1) % QT]):
                        pt_low(g - 1, r)
                before_scores = early(g) and g % 2
                if early(g):
                    v_value(g + 1)
                if before_scores and g + AHEAD + 1 < STEPS:
                    normalise(g + AHEAD + 1)
                if g == STEPS - CT:
                    prep.statistics(dve, 0)
                if g == STEPS - CT + 1:
                    prep.normalise(dve, 0)
                if g == STEPS - 1:
                    prep.top_two(dve, 0, prep_bank)
                short = g % QT <= CT and g < STEPS
                if short:
                    maximum(g)
                    exp_bias(g)
                if not before_scores and g + AHEAD + 1 < STEPS:
                    normalise(g + AHEAD + 1)
                if g % 2 and g + 1 < STEPS:
                    y_low((g + 1) // 2)
                if not early(g) and g + AHEAD < STEPS:
                    xt_low(g + AHEAD)
                if g == STEPS - 2:
                    for k in range(KD):
                        prep.xt_low(dve, 0, 0, k, prep_banks[k])
                if not short and g < STEPS:
                    maximum(g)
                    exp_bias(g)
                if g > 0:
                    inverse(g - 1)
                if g == STEPS - 2:
                    prep.statistics(dve, 1)
                if g + AHEAD + 2 < STEPS:
                    statistics(g + AHEAD + 2)
                if g == STEPS:
                    prep.normalise(dve, 1)
                if g > 0 and (g == STEPS or not early(g + 1)):
                    residual(g - 1)

        @block.tensor
        def _(pe):
            def group(out, pairs):
                for n, (a, b) in enumerate(pairs):
                    last = nc.tensor.matmul(out, a, b, start=n == 0, stop=n == len(pairs) - 1)
                return last

            def transposes(t):
                n, g = t - CT, t - AHEAD
                if g % 2 and other_pt(g):
                    need(pe, pt_lo_done, group0(g) - 1)
                elif g % 2:
                    pe.wait_ge(v_f_done, g + 2)
                else:
                    need(pe, exp_done, g - early(g))
                pe.wait_ge(xn_done, n + 1)
                for k in range(KD):
                    last = nc.tensor.transpose(t_ps(t)[:, k * P:(k + 1) * P], xn[:, n % 2, k * P:(k + 1) * P], ident[:, :])
                last.then_inc(t_made, 1)

            def y(p):
                need(pe, exp_done, 2 * p - 1)
                need(pe, xt_lo_done, 2 * p + 2 - CT)
                four, _ = place(2 * p)
                cols = slice(2 * p % CT * P, (2 * p % CT + 2) * P)
                for m in range(KD):
                    pairs = [(a[:, k, m * P:(m + 1) * P], t[:, four, k, cols])
                             for a, t in split_terms(a_hi, a_lo, xt_hi, xt_lo) for k in range(KD)]
                    last = group(y_ps(p, m), pairs)
                last.then_inc(y_made, 1)

            def v(t):
                four, cols = place(t)
                need(pe, v_f_done, t)
                need(pe, xt_lo_done, min((t - 1) // 2 * 2, STEPS - CT))
                pairs = [(a[:, four, k, cols], w[:, k, :])
                         for a, w in split_terms(xt_hi, xt_lo, b_hi, b_lo) for k in range(KD)]
                group(v_ps[:, 0:VW], pairs).then_inc(v_made, 1)

            def scores(g):
                i = g % QT
                need(pe, exp_done, g - 1)
                pe.wait_ge(y_lo_done, g // 2 + 1)
                need(pe, xt_lo_done, min(g, STEPS - CT))
                n = (i + 1) * P
                here = slice(i % 2 * P, (i % 2 + 1) * P)
                for c0 in range(0, n, CN):
                    width = min(CN, max(n - c0, 2 * P))
                    four, _ = place(g - i + c0 // P)
                    pairs = [(a[:, g // 2 % 2, k, here], t[:, four, k, 0:width])
                             for a, t in split_terms(yt_hi, yt_lo, xt_hi, xt_lo) for k in range(KD)]
                    for m, (q, keys) in enumerate(pairs):
                        nc.tensor.matmul(s_ps[g % 2][:, c0:c0 + width], q, keys, start=m == 0, stop=False,
                                         skip_group_check=True)
                last = nc.tensor.matmul(s_ps[g % 2][:, n - P:n], consts["ident_b"][:, :], consts["mask_b"][:, :],
                                        start=False, stop=True, skip_group_check=True)
                last.then_inc(s_made, 1)

            def prob_transposes(g):
                i = g % QT
                pe.wait_ge(exp_done, g + 1)
                need(pe, xt_lo_done, min(g + 1, STEPS - CT))
                for r in range(groups[i]):
                    G = group0(g) + r
                    need(pe, pt_lo_done, G - 1)
                    for k in range(r * CT, min(i + 1, (r + 1) * CT)):
                        last = nc.tensor.transpose(pt_ps[G % 2][:, (k - r * CT) * P:(k - r * CT + 1) * P],
                                                   prob[:, g % 2, k * P:(k + 1) * P], ident[:, :])
                    last.then_inc(pt_made, 1)

            def values(g):
                i = g % QT
                need(pe, x_done, g)
                pe.wait_ge(v_done, g + 1)
                for k in range(i + 1):
                    if k % CT == 0:
                        pe.wait_ge(pt_lo_done, group0(g) + k // CT + 1)
                    slot = (g - i + k) % VR
                    for m, (p, w) in enumerate(split_terms(pt_hi, pt_lo, v_hi, v_lo)):
                        last = nc.tensor.matmul(pv_ps, p[:, k, :], w[:, slot, :], start=k + m == 0,
                                                stop=k == i and m == 2)
                last.then_inc(pv_made, 1)

            pe.wait_ge(first.xt_lo_done, 1)
            v(0)
            y(0)

            for g in range(STEPS):
                if g == STEPS - 1:
                    prep.logits(pe, 0, 0, prep_bank)
                if g + 1 < STEPS:
                    v(g + 1)
                if early(g) and g + AHEAD < STEPS:
                    transposes(g + AHEAD)
                if g > 0:
                    prob_transposes(g - 1)
                if g == STEPS - 1:
                    prep.logits_by_token(pe, 0, prep_bank)
                if g % 2 and g + 1 < STEPS:
                    y((g + 1) // 2)
                if g == 0:
                    pe.wait_ge(first.xt_lo_done, len(firsts))
                if not early(g) and g + AHEAD < STEPS:
                    transposes(g + AHEAD)
                if g == STEPS - 2:
                    pe.wait_ge(v_f_done, STEPS)
                    for k in range(KD):
                        prep.transpose(0, k, prep_banks[k])
                scores(g)
                if g > 0:
                    values(g - 1)
            prob_transposes(STEPS - 1)
            prep.weights_by_feature(pe, 0, prep_bank)
            values(STEPS - 1)


def build(nc, a, out):
    with ExitStack() as ctx:
        def sb(n, shape, dt=F32):
            return ctx.enter_context(nc.sbuf_tensor(n, shape, dt))
        x = sb("x", [P, TILES, D])
        consts = {
            "ident": sb("ident", [P, P]),
            "sel": sb("sel", [2 * E, FB, P], F32R),
            "iota": sb("iota", [P, CT * E]),
            "mhalf": sb("mhalf", [P, CT]),
            "eps": sb("eps", [P, CT]),
            "ident_b": sb("ident_b", [P, P], BF16), "mask_b": sb("mask_b", [P, P], BF16),
        }
        w = {
            "gu_hi": sb("gu_hi", [P, KD, 2 * F], F32R), "gu_lo": sb("gu_lo", [P, KD, 2 * F], F32R),
            "dn_hi": sb("dn_hi", [P, FB, D], F32R), "dn_lo": sb("dn_lo", [P, FB, D], F32R),
            "rt": sb("rt", [P, KD, 2 * E], F32R),
        }
        aw = {
            "wq": sb("wq", [P, NG, D]), "wk": sb("wk", [P, NG, D + 1]), "wv": sb("wv", [P, NG, D]),
            "proj": sb("proj", [P, NG, D]),
            "bq": sb("bq", [P, R, NG]), "bk": sb("bk", [P, NG]), "bv": sb("bv", [P, NG]),
        }
        repeats = {n: a[n].rearrange("(r g h) d -> r h g d", h=P, g=NG) for n in ("wq", "proj")}
        attn = {
            "wq": (aw["wq"][:, :, :], repeats["wq"][0]), "proj": (aw["proj"][:, :, :], repeats["proj"][0]),
            "wq_repeats": repeats["wq"], "proj_repeats": repeats["proj"],
            "wk": (aw["wk"][:, :, 0:D], a["wk"].rearrange("(g h) d -> h g d", h=P)),
            "wv": (aw["wv"][:, :, :], a["wv"].rearrange("(g h) d -> h g d", h=P)),
            "bq": (aw["bq"][:, :, :], a["bq"]), "bk": (aw["bk"][:, :], a["bk"]), "bv": (aw["bv"][:, :], a["bv"]),
        }
        load = {
            "attn": attn,
            "x": a["x"].rearrange("b (n p) d -> p (b n) d", p=P),
            "w_gate": a["w_gate"].rearrange("(k p) f -> p k f", p=P),
            "w_up": a["w_up"].rearrange("(k p) f -> p k f", p=P),
            "w_down": a["w_down"].rearrange("(k p) f -> p k f", p=P),
            "w_router": a["w_router"].rearrange("(k p) e -> p k e", p=P),
            "sel": a["sel"], "iota": a["iota"], "ident": a["ident"],
            "ident_b": a["ident_b"], "mask_b": a["mask_b"],
        }
        banks = {
            "s": [ctx.enter_context(nc.psum_tensor(f"s{i}", [P, T], F32)) for i in range(2)],
            "q": [ctx.enter_context(nc.psum_tensor(f"q{i}", [P, CN], F32)) for i in range(4)],
        }

        def sem(n):
            return ctx.enter_context(nc.semaphore(n))

        warm_in, warm_out = sb("warm_in", [P, 1]), sb("warm_out", [P, 1])
        warm = {"in": warm_in[:, :], "out": warm_out[:, :], "set": sem("warm_set")}
        buf = prep_buffers(sb)
        fold = Fold(nc, aw, banks, sb, sem)
        moe1_prep, first, moe2_prep = (Prep(nc, x, consts, w, buf, lambda s, n=n: sem(f"{n}_{s}"), x_in)
                                       for n, x_in in (("prep1", sem("x_in")), ("first", None), ("prep2", None)))
        moe_phase(nc, "moe1", x, consts, w, banks, moe1_prep, warm, load=load, fold=fold, after=first)
        attention_phase(nc, x, consts, fold, banks, warm, first, moe2_prep)
        out_t = out.rearrange("b (n p) d -> p (b n) d", p=P)
        moe_phase(nc, "moe2", x, consts, w, banks, moe2_prep, warm, store={"out": out_t, "sem": sem("stored")})


def kernel(**inputs):
    import concourse.bacc as bacc
    from concourse.bass_utils import run_bass_kernel_spmd

    bf16 = mybir.dt.np(BF16)
    g = {k: np.asarray(v) for k, v in inputs.items()}
    experts = np.arange(F) // FE
    sel = (experts[None, :] == (np.arange(2 * E) % E)[:, None]).astype(np.float32)
    arrays = {
        "x": g["L0_attn_x"],
        "w_gate": g["L0_ffn_w_gate_proj"].reshape(F, D).T,
        "w_up": g["L0_ffn_w_up_proj"].reshape(F, D).T,
        "w_down": g["L0_ffn_w_down_proj"].transpose(0, 2, 1).reshape(F, D),
        "w_router": g["L0_ffn_w_gate_router"].T,
        "wq": g["L0_attn_WQ"], "wk": g["L0_attn_WK"], "wv": g["L0_attn_WV"], "proj": g["L0_attn_proj"],
        "bq": g["L0_attn_bQ"].reshape(R, NG, P).transpose(2, 0, 1),
        "bk": g["L0_attn_bK"].reshape(NG, P).T, "bv": g["L0_attn_bV"].reshape(NG, P).T,
        "ident_b": np.eye(P, dtype=np.float32).astype(bf16),
        "mask_b": np.triu(np.full((P, P), MASKED, np.float32), 1).astype(bf16),
        "sel": sel.reshape(2 * E, FB, P).astype(bf16),
        "iota": np.tile(np.arange(E, dtype=np.float32), (P, CT)),
        "ident": np.eye(P, dtype=np.float32),
    }
    nc = bacc.Bacc("TRN2", target_bir_lowering=False, num_devices=1)
    in_map, a = {}, {}
    for name, value in arrays.items():
        value = np.ascontiguousarray(value)
        in_map[f"in_{name}"] = value
        a[name] = nc.dram_tensor(f"in_{name}", value.shape, mybir.dt.from_np(value.dtype), kind="ExternalInput").ap()
    out = nc.dram_tensor("out", (B, T, D), F32, kind="ExternalOutput").ap()
    build(nc, a, out)
    r = run_bass_kernel_spmd(nc, [in_map], core_ids=[0])
    return r.results[0]["out"]
```
